# Optimizing a Trainium2 kernel written in Bass

```python
import numpy as np
import jax
import jax.numpy as jnp

def _softmax(x, axis=-1):
    return jax.nn.softmax(x, axis=axis)

def _gelu(x):
    return jax.nn.gelu(x, approximate=True)

def _silu(x):
    return jax.nn.silu(x)

def _sigmoid(x):
    return jax.nn.sigmoid(x)

def _layernorm(x, axis=-1, eps=1e-05):
    m = jnp.mean(x, axis=axis, keepdims=True)
    v = jnp.var(x, axis=axis, keepdims=True)
    return (x - m) / jnp.sqrt(v + eps)

def _scatter_add(tgt, idx, src, axis=0):
    return tgt.at[idx].add(src)

def _segment_sum(src, seg, n):
    return jax.ops.segment_sum(src, seg, n)
kernel_name = 'mk_vit_tower_d1_tok_img768_r4_97742f'

def setup_inputs(seed: int=0):
    np.random.seed(seed)
    _w = jnp.asarray

    def _rec_inputs():
        import jax
        import jax.numpy as jnp
        _rk = jax.random.key(seed)
        x = -0.000363531 + 1.00001 * jax.random.normal(jax.random.fold_in(_rk, 1), (64, 4, 137, 137), jnp.float32)
        return x
    x = _rec_inputs()

    def _L0_tok_setup():
        import jax, jax.numpy as jnp
        import numpy as np
        B, C, H, W_IMG = (64, 4, 137, 137)
        K = 13
        PG = 11
        N = PG * PG
        D_IN = C * K * K
        D = 192

        def _patchify(x):
            x = jnp.pad(x, ((0, 0), (0, 0), (3, 3), (3, 3)))
            x = x.reshape(x.shape[0], C, PG, K, PG, K)
            x = x.transpose(0, 2, 4, 1, 3, 5)
            return x.reshape(x.shape[0], N, D_IN)
        key = jax.random.key(seed)
        k1, k2, k3, k4 = jax.random.split(key, 4)
        images = jax.random.normal(k1, (B, C, H, W_IMG), dtype=jnp.float32)
        W = jax.random.normal(k2, (D, D_IN), dtype=jnp.float32) * (1.0 / np.sqrt(D_IN))
        b = jax.random.normal(k3, (D,), dtype=jnp.float32) * 0.02
        pos_emb = jax.random.normal(k4, (N, D), dtype=jnp.float32)
        return {'images': images, 'W': W, 'b': b, 'pos_emb': pos_emb}
    _L0_tok_all = _L0_tok_setup()
    _L0_tok_in = {k: v for k, v in _L0_tok_all.items() if k in ('W', 'b', 'pos_emb')}
    del _L0_tok_all

    def _L0_attn_setup():
        import jax, jax.numpy as jnp
        import numpy as np
        NHEAD = 12
        EPS = 1e-05

        def layernorm_nobias(x, gamma):
            mu = jnp.mean(x, axis=-1, keepdims=True)
            var = jnp.var(x, axis=-1, keepdims=True)
            return (x - mu) * jax.lax.rsqrt(var + EPS) * gamma
        key = jax.random.key(seed)
        ks = jax.random.split(key, 10)
        b, l, d = (4, 512, 192)
        s = d ** (-0.5)
        return {'x': jax.random.normal(ks[0], (b, l, d), jnp.float32), 'Wq': jax.random.normal(ks[1], (d, d), jnp.float32) * s, 'Wk': jax.random.normal(ks[2], (d, d), jnp.float32) * s, 'bk': jax.random.normal(ks[3], (d,), jnp.float32) * 0.02, 'Wv': jax.random.normal(ks[4], (d, d), jnp.float32) * s, 'bv': jax.random.normal(ks[5], (d,), jnp.float32) * 0.02, 'gq': jnp.ones((d,), jnp.float32), 'gk': jnp.ones((d,), jnp.float32), 'Wo': jax.random.normal(ks[6], (d, d), jnp.float32) * s, 'bo': jnp.zeros((d,), jnp.float32)}
    _L0_attn_all = _L0_attn_setup()
    _L0_attn_in = {k: v for k, v in _L0_attn_all.items() if k in ('Wq', 'Wk', 'bk', 'Wv', 'bv', 'gq', 'gk', 'Wo', 'bo')}
    del _L0_attn_all

    def _L0_ffn_setup():
        import jax, jax.numpy as jnp
        import numpy as np
        B, S, D, E, K = (1, 256, 192, 8, 2)
        H = 4 * D
        key = jax.random.key(seed)
        ks = jax.random.split(key, 6)
        s = jnp.float32(0.02)
        return {'x': jax.random.normal(ks[0], (B, S, D), jnp.float32), 'Wr': jax.random.normal(ks[1], (E, D), jnp.float32) * s, 'W1': jax.random.normal(ks[2], (E, H, D), jnp.float32) * s, 'b1': jnp.zeros((E, H), jnp.float32), 'W2': jax.random.normal(ks[3], (E, D, H), jnp.float32) * s, 'b2': jnp.zeros((E, D), jnp.float32), 'sW1': jax.random.normal(ks[4], (H, D), jnp.float32) * s, 'sb1': jnp.zeros((H,), jnp.float32), 'sW2': jax.random.normal(ks[5], (D, H), jnp.float32) * s, 'sb2': jnp.zeros((D,), jnp.float32)}
    _L0_ffn_all = _L0_ffn_setup()
    _L0_ffn_in = {k: v for k, v in _L0_ffn_all.items() if k in ('Wr', 'W1', 'b1', 'W2', 'b2', 'sW1', 'sb1', 'sW2', 'sb2')}
    del _L0_ffn_all
    return {'x': x, 'L0_tok_W': _L0_tok_in['W'], 'L0_tok_b': _L0_tok_in['b'], 'L0_tok_pos_emb': _L0_tok_in['pos_emb'], 'L0_attn_Wq': _L0_attn_in['Wq'], 'L0_attn_Wk': _L0_attn_in['Wk'], 'L0_attn_bk': _L0_attn_in['bk'], 'L0_attn_Wv': _L0_attn_in['Wv'], 'L0_attn_bv': _L0_attn_in['bv'], 'L0_attn_gq': _L0_attn_in['gq'], 'L0_attn_gk': _L0_attn_in['gk'], 'L0_attn_Wo': _L0_attn_in['Wo'], 'L0_attn_bo': _L0_attn_in['bo'], 'L0_ffn_Wr': _L0_ffn_in['Wr'], 'L0_ffn_W1': _L0_ffn_in['W1'], 'L0_ffn_b1': _L0_ffn_in['b1'], 'L0_ffn_W2': _L0_ffn_in['W2'], 'L0_ffn_b2': _L0_ffn_in['b2'], 'L0_ffn_sW1': _L0_ffn_in['sW1'], 'L0_ffn_sb1': _L0_ffn_in['sb1'], 'L0_ffn_sW2': _L0_ffn_in['sW2'], 'L0_ffn_sb2': _L0_ffn_in['sb2']}

def reference(x, L0_tok_W, L0_tok_b, L0_tok_pos_emb, L0_attn_Wq, L0_attn_Wk, L0_attn_bk, L0_attn_Wv, L0_attn_bv, L0_attn_gq, L0_attn_gk, L0_attn_Wo, L0_attn_bo, L0_ffn_Wr, L0_ffn_W1, L0_ffn_b1, L0_ffn_W2, L0_ffn_b2, L0_ffn_sW1, L0_ffn_sb1, L0_ffn_sW2, L0_ffn_sb2):
    import jax
    import jax.numpy as jnp

    def _L0_tok_ref(images, W, b, pos_emb):
        import jax, jax.numpy as jnp
        import numpy as np
        B, C, H, W_IMG = (64, 4, 137, 137)
        K = 13
        PG = 11
        N = PG * PG
        D_IN = C * K * K
        D = 192

        def _patchify(x):
            x = jnp.pad(x, ((0, 0), (0, 0), (3, 3), (3, 3)))
            x = x.reshape(x.shape[0], C, PG, K, PG, K)
            x = x.transpose(0, 2, 4, 1, 3, 5)
            return x.reshape(x.shape[0], N, D_IN)
        patches = _patchify(images)
        emb = jnp.einsum('bnf,df->bnd', patches, W) + b
        return emb + pos_emb[None, :, :]

    def _L0_attn_ref(x, Wq, Wk, bk, Wv, bv, gq, gk, Wo, bo):
        import jax, jax.numpy as jnp
        import numpy as np
        NHEAD = 12
        EPS = 1e-05

        def layernorm_nobias(x, gamma):
            mu = jnp.mean(x, axis=-1, keepdims=True)
            var = jnp.var(x, axis=-1, keepdims=True)
            return (x - mu) * jax.lax.rsqrt(var + EPS) * gamma
        b, l, d = x.shape
        n = NHEAD
        hd = d // n
        scale = hd ** (-0.5)
        q = layernorm_nobias(x @ Wq.T, gq)
        k = layernorm_nobias(x @ Wk.T + bk, gk)
        v = x @ Wv.T + bv
        q = q.reshape(b, l, n, hd).transpose(0, 2, 1, 3)
        k = k.reshape(b, l, n, hd).transpose(0, 2, 1, 3)
        v = v.reshape(b, l, n, hd).transpose(0, 2, 1, 3)
        scores = jnp.einsum('bnqd,bnkd->bnqk', q, k) * scale
        attn = jax.nn.softmax(scores, axis=-2)
        o = jnp.einsum('bnqk,bnkd->bnqd', attn, v)
        o = o.transpose(0, 2, 1, 3).reshape(b, l, d)
        return o @ Wo.T + bo + x

    def _L0_ffn_ref(x, Wr, W1, b1, W2, b2, sW1, sb1, sW2, sb2):
        import jax, jax.numpy as jnp
        import numpy as np
        B, S, D, E, K = (1, 256, 192, 8, 2)
        H = 4 * D
        Bx, Sx, Dx = x.shape
        xf = x.reshape(-1, Dx)
        T = xf.shape[0]
        logits = xf @ Wr.T
        topv, idx = jax.lax.top_k(logits, K)
        gate_k = jax.nn.softmax(topv, axis=-1)
        gates = jnp.zeros((T, logits.shape[-1]), x.dtype).at[jnp.arange(T)[:, None], idx].add(gate_k)
        h = jax.nn.relu(jnp.einsum('td,ehd->teh', xf, W1) + b1)
        y = jnp.einsum('teh,edh->ted', h, W2) + b2
        moe = jnp.einsum('te,ted->td', gates, y)
        sh = jax.nn.relu(xf @ sW1.T + sb1) @ sW2.T + sb2
        out = moe + 0.1 * K * sh
        return out.reshape(Bx, Sx, Dx)
    h = _L0_tok_ref(x, L0_tok_W, L0_tok_b, L0_tok_pos_emb)
    h = h + _L0_attn_ref(_layernorm(h, axis=-1), L0_attn_Wq, L0_attn_Wk, L0_attn_bk, L0_attn_Wv, L0_attn_bv, L0_attn_gq, L0_attn_gk, L0_attn_Wo, L0_attn_bo)
    h = h + _L0_ffn_ref(_layernorm(h, axis=-1), L0_ffn_Wr, L0_ffn_W1, L0_ffn_b1, L0_ffn_W2, L0_ffn_b2, L0_ffn_sW1, L0_ffn_sb1, L0_ffn_sW2, L0_ffn_sb2)
    return h

_drawn_inputs = setup_inputs


def setup_inputs(seed=0):
    import zlib

    import numpy as np

    out = dict(_drawn_inputs(seed))
    spreads = {'L0_attn_gq': (1.0, 0.6),
     'L0_attn_gk': (1.0, 0.6),
     'L0_attn_bo': (0.0, 0.1),
     'L0_ffn_b1': (0.0, 0.705),
     'L0_ffn_b2': (0.0, 0.269),
     'L0_ffn_sb1': (0.0, 0.8),
     'L0_ffn_sb2': (0.0, 0.8)}
    factors = {'L0_tok_b': 3.281,
     'L0_attn_bk': 8.0,
     'L0_attn_bv': 5.374,
     'L0_ffn_sW1': 7.329,
     'L0_ffn_sW2': 5.754}
    for name, (base, spread) in spreads.items():
        noise = np.random.default_rng([zlib.crc32(name.encode()), seed]).standard_normal(out[name].shape)
        drawn = base * np.exp(spread * noise) if base else spread * noise
        out[name] = jnp.asarray(drawn.astype(out[name].dtype))
    for name, factor in factors.items():
        out[name] = (out[name] * factor).astype(out[name].dtype)
    return out
```

```python
from contextlib import ExitStack

import concourse.bass as bass
from concourse import mybir

F32 = mybir.dt.float32
F32R = mybir.dt.float32r
U32 = mybir.dt.uint32
ALU = mybir.AluOpType
ACT = mybir.ActivationFunctionType
AX = mybir.AxisListType.X

P = 128
B = 64
N = 121
T = B * N
D = 192
DH = D // 2
NH = 12
HD = 16
NG = NH // 4
NE = 8
H = 768
MH = H // P
KE = 6
EPS = 1e-5
HSCALE = float(HD) ** -0.5
MOE_SCALE = 0.2

GROUPS = 4
TS = GROUPS * P
CAP = T + TS
NSLOT = (2 * T + NE * (TS - 1)) // TS
NTHR = -(-T // TS)
SH = 16
SR = T // SH // GROUPS
SE = SR + SR % 2
W1C, W2C = 3 * H, MH * D

NALL = NSLOT + SH
assert NSLOT % 2 == 0 and NALL % 2 == 0
TAB = 16

C_ID = 0
C_TRI = C_ID + P
C_IOTA = C_TRI + P
C_CAP = C_IOTA + NE
C_THR = C_CAP + NE
C_SLOT = C_THR + NTHR
C_LE = C_SLOT + NSLOT
C_BIAS = C_LE + NE * NE
C_END = C_BIAS + 1


class Image:

    def __init__(self, q, off, least=None):
        self.q, self.off = q, off
        self.fixed = least is None
        self.least = 4 * (q if self.fixed else least) + off
        self.n = 4 * q + off
        self.m4, self.m2, self.pair = off % 4, off % 2, (off // 2) % 2
        self.quad = q + off // 4
        self.half = 2 * q + off // 2

    def valid(self):
        return not self.fixed or 0 <= self.n < B

    def since(self, k):
        assert self.fixed or self.least >= k
        return self.least >= k


class Slot:

    def __init__(self, q, off, least=None):
        self.fixed = least is None
        self.least = 2 * (q if self.fixed else least) + off
        self.n = 2 * q + off
        self.par = off % 2
        self.half = q + off // 2
        self.routed = self.least < NSLOT
        self.k = self.n - NSLOT
        self.khalf = self.half - NSLOT // 2
        self.wn = self.n if self.routed else NSLOT
        self.wpar = self.par if self.routed else 0
        self.whalf = self.half if self.routed else NSLOT // 2
        self.rows = P if self.routed else SE
        self.cols = GROUPS * self.rows

    def valid(self):
        return not self.fixed or 0 <= self.n < NALL

    def weights(self):
        return self.least <= NSLOT

    def since(self, k):
        assert self.fixed or self.least >= k or not self.routed or k > NSLOT
        return self.least >= k

    def tokens(self, rows):
        return rows[bass.ds(self.k * (SR * GROUPS), SR * GROUPS), :].rearrange("(p g) d -> p g d", g=GROUPS)


def build(nc, a):
    ctx = ExitStack()
    with ctx:
        def sb(name, shape, dt=F32, c=ctx):
            return c.enter_context(nc.sbuf_tensor(name, shape, dt))

        def sem(name):
            return ctx.enter_context(nc.semaphore(name))

        banks = [ctx.enter_context(nc.psum_tensor(f"bank{i}", [P, 512], F32)) for i in range(8)]

        wo_ps, pre_ps, lg_ps = banks[6][0:N, 0:D], banks[6][0:N, 0:2 * NE], banks[6][0:N, 0:NE]
        emb_ps, v_ps = banks[7][0:N, 0:D], banks[5][0:N, 0:D]
        cnt_ps = banks[7][:, 0:NE]

        xs_rows = nc.dram_tensor("xs_rows", [NE * CAP, D], F32, kind="Internal").ap()
        y_rows = nc.dram_tensor("y_rows", [NSLOT * TS, D], F32, kind="Internal").ap()
        xf_rows = nc.dram_tensor("xf_rows", [T, D], F32, kind="Internal").ap()
        h2_rows = nc.dram_tensor("h2_rows", [T, D], F32, kind="Internal").ap()
        meta_rows = nc.dram_tensor("meta_rows", [T, 4], F32, kind="Internal").ap()

        consts = sb("consts", [P, C_END])
        ident = consts[:, C_ID:C_ID + P]
        tri = consts[0:N, C_TRI:C_TRI + N]
        identr = sb("identr", [P, P], F32R)
        ones = sb("ones", [P, P])
        cmask = sb("cmask", [N, 2, 2, NE])
        table = sb("table", [1, 2, NSLOT], U32)
        zrow = sb("zrow", [1, NE], U32)

        w1raw = sb("w1raw", [P, W1C])
        w2raw = sb("w2raw", [P, W2C])
        b1 = sb("b1", [P, 2, MH])
        b2 = sb("b2", [P, 2, D])
        xr = sb("xr", [P, 2, GROUPS, D])
        xsplit = sb("xsplit", [P, GROUPS, 2 * D], F32R)
        xT = sb("xT", [P, 2, 3, TS], F32R)
        hf = sb("hf", [P, 2, TS])
        ysb = sb("ysb", [P, 2, GROUPS, D])

        ztile = sb("ztile", [P, GROUPS * D])
        cnt = sb("cnt", [P, NE])
        tcmp = sb("tcmp", [P, NE, NTHR])
        nsl = sb("nsl", [P, NE])
        tcum = sb("tcum", [1, NE, NE])
        cum = sb("cum", [1, NE])
        step8 = sb("step8", [P, NE])
        past = sb("past", [1, NSLOT, NE])
        tmul = sb("tmul", [1, NSLOT, NE])
        tsum = sb("tsum", [1, 5, NSLOT])

        one = ExitStack()
        we = sb("we", [P, KE, D], F32, one)
        wqkv = sb("wqkv", [DH + 1, 2, 3 * D], F32, one)
        wo = sb("wo", [P, NG, D], F32, one)
        wr = sb("wr", [DH, 2, NE], F32, one)
        gains = sb("gains", [P, 2, NG], F32, one)
        gain = sb("gain", [P, NG], F32, one)
        posb = sb("posb", [N, 2, D], F32, one)
        mhalf = sb("mhalf", [N, 2], F32, one)
        xin = sb("xin", [P, 2, KE, N], F32, one)
        h = sb("h", [N, 2, D], F32, one)
        xln = sb("xln", [N, 2, D], F32, one)
        hx = sb("hx", [N, 4, D], F32, one)
        st1 = sb("st1", [N, 2, 6], F32, one)
        mv1 = sb("mv1", [N, 2, 2], F32, one)
        ve1 = sb("ve1", [N, 2, 1], F32, one)
        rs1 = sb("rs1", [N, 2, 1], F32, one)
        stq = sb("stq", [N, 2, 2, 6], F32, one)
        mvq = sb("mvq", [N, 2, 2, 2], F32, one)
        veq = sb("veq", [N, 2, 2], F32, one)
        rsq = sb("rsq", [N, 2, 2], F32, one)
        st2 = sb("st2", [N, 2, 6], F32, one)
        mv2 = sb("mv2", [N, 2, 2], F32, one)
        ve2 = sb("ve2", [N, 2, 1], F32, one)
        rs2 = sb("rs2", [N, 2, 1], F32, one)
        xlnT = sb("xlnT", [DH + 1, 2, 2, N], F32, one)
        qpad = sb("qpad", [N, 2, NH, 32], F32, one)
        kpad = sb("kpad", [N, 2, NH, 32], F32, one)
        qT = sb("qT", [P, 2, NG, N], F32, one)
        kT = sb("kT", [P, 2, NG, N], F32, one)
        vsb = sb("vsb", [N, 2, D], F32, one)
        vn = sb("vn", [N, 2, NH, 32], F32, one)
        negmax = sb("negmax", [N, 2, NH], F32, one)
        rowsum = sb("rowsum", [N, 2, NH], F32, one)
        rinv = sb("rinv", [N, 2, NH], F32, one)
        probs = sb("probs", [N, 2, NH, N], F32, one)
        oT = sb("oT", [P, 2, NG, N], F32, one)
        h2 = sb("h2", [N, 2, D], F32, one)
        xf = sb("xf", [N, 4, D], F32, one)
        xfT = sb("xfT", [DH, 2, 2, N], F32, one)
        lg = sb("lg", [N, 2, 2, NE], F32, one)
        top = sb("top", [N, 2, 2, NE], F32, one)
        topi = sb("topi", [N, 2, 2, NE], U32, one)
        hot = sb("hot", [N, 2, 2, 2, NE], F32, one)
        mask = sb("mask", [N, 2, 2, NE], F32, one)
        place = sb("place", [N, 2, 2, NE], F32, one)
        picked = sb("picked", [N, 2, 2, 2, NE], F32, one)
        meta = sb("meta", [N, 2, 2, 4], F32, one)
        dest = sb("dest", [N, 2, 2, 2], U32, one)
        one.close()
        w1h = sb("w1h", [P, 2, W1C], F32R)
        w1l = sb("w1l", [P, 2, 2 * H], F32R)
        w2h = sb("w2h", [P, 2, W2C], F32R)
        w2l = sb("w2l", [P, 2, W2C], F32R)
        hh = sb("hh", [P, 2, MH, TS], F32R)
        hl = sb("hl", [P, 2, MH, TS], F32R)
        acc = sb("acc", [SR, 2, GROUPS, D])
        ye = sb("ye", [SR, 2, 2, GROUPS, D])
        mrow = sb("mrow", [SR, 2, GROUPS, 4])
        gidx = sb("gidx", [SR, 2, GROUPS, 2], U32)
        behind = sb("behind", [SR, GROUPS, 2, NE - 1])
        moved = sb("moved", [SR, GROUPS, 2])
        gate = sb("gate", [SR, 2, 5, GROUPS])

        ld_w = sem("ld_w")
        ld_x = [sem(f"ld_x{i}") for i in range(2)]
        st_h2 = [sem(f"st_h2{i}") for i in range(2)]
        st_xf = [sem(f"st_xf{i}") for i in range(4)]
        st_meta = [sem(f"st_meta{i}") for i in range(2)]
        scat = [sem(f"scat{i}") for i in range(4)]
        ps_emb, ps_q, ps_k, ps_av, ps_qk, ps_v, ps_sc, ps_xfT, ps_xlnT, ps_wo, ps_lg, ps_pre = (
            sem(n) for n in ("ps_emb", "ps_q", "ps_k", "ps_av", "ps_qk", "ps_v", "ps_sc", "ps_xfT",
                             "ps_xlnT", "ps_wo", "ps_lg", "ps_pre"))
        sb_q, sb_k, sb_v, sb_oT, sb_xfT, sb_xlnT, exps = (
            sem(n) for n in ("sb_q", "sb_k", "sb_v", "sb_oT", "sb_xfT", "sb_xlnT", "exps"))
        d_ln1, d_qk, d_max, d_v, d_ln2, d_lg, d_route = (
            sem(n) for n in ("d_ln1", "d_qk", "d_max", "d_v", "d_ln2", "d_lg", "d_route"))
        p_rs1, p_rsq, p_rs2, p_hx = (sem(n) for n in ("p_rs1", "p_rsq", "p_rs2", "p_hx"))
        dve_passed, pool_passed = sem("dve_passed"), sem("pool_passed")
        init_v, init_p = sem("init_v"), sem("init_p")
        ps_cnt, d_tab, st_zero = sem("ps_cnt"), sem("d_tab"), sem("st_zero")
        ld_w1, ld_w2 = sem("ld_w1"), sem("ld_w2")
        ld_b1, ld_b2, ld_xr, ld_meta, ld_h2, st_y, gath = (
            [sem(f"{n}{i}") for i in range(2)] for n in ("ld_b1", "ld_b2", "ld_xr", "ld_meta", "ld_h2", "st_y", "gath"))
        w1_hi, w1_lo, w2_hi, w2_lo = (sem(n) for n in ("w1_hi", "w1_lo", "w2_hi", "w2_lo"))
        d_xs, ps_T, sb_T, ps_h, sb_h, d_h, ps_y, d_y, d_out = (
            sem(n) for n in ("d_xs", "ps_T", "sb_T", "ps_h", "sb_h", "d_h", "ps_y", "d_y", "d_out"))
        d_idx, a_gate, d_gate, d_acc = (sem(n) for n in ("d_idx", "a_gate", "d_gate", "d_acc"))
        LN1, QKN, LN2, ROUTE = 5, 7, 5, 15

        def phase1_over(eng):
            for i in range(4):
                eng.wait_ge(scat[i], 32 * B // 4)
                eng.wait_ge(st_xf[i], 16 * B // 4)
            for i in range(2):
                eng.wait_ge(st_h2[i], 16 * B // 2)
                eng.wait_ge(st_meta[i], 16 * B // 4)
            eng.wait_ge(exps, NH * B)
            eng.wait_ge(sb_xfT, B)
            eng.wait_ge(ps_cnt, 1)
            eng.wait_ge(d_route, ROUTE * B // 2)
            eng.wait_ge(p_rs2, B)

        def slots(eng, step):
            def straight(q0, q1):
                for q in range(q0, q1):
                    for u in range(2):
                        step(lambda d, q=q, u=u: Slot(q, u + d))

            def loop(q0, q1):
                with eng.Fori(q0, q1) as q:
                    for u in range(2):
                        step(lambda d, q=q, u=u: Slot(q, u + d, q0))

            straight(-2, 1)
            loop(1, NSLOT // 2 - 2)
            straight(NSLOT // 2 - 2, NSLOT // 2 + 1)
            loop(NSLOT // 2 + 1, NALL // 2 - 2)
            straight(NALL // 2 - 2, NALL // 2)

        def phase2_sp(sp):
            sp.wait_ge(d_tab, TAB)
            sp.wait_ge(init_p, 7)
            for i in range(4):
                sp.wait_ge(scat[i], 32 * B // 4)
            for e in range(NE):
                row = sp.value_load(zrow[0:1, e:e + 1], min_val=0, max_val=NE * CAP - TS)
                sp.dma_start(xs_rows[bass.ds(row, TS), :].rearrange("(p g) d -> p (g d)", g=GROUPS), ztile[:])\
                    .then_inc(st_zero, 16)
            sp.wait_ge(st_zero, 16 * NE)
            for i in range(4):
                sp.wait_ge(st_xf[i], 16 * B // 4)
            for i in range(2):
                sp.wait_ge(st_h2[i], 16 * B // 2)
                sp.wait_ge(st_meta[i], 16 * B // 4)
            phase1_over(sp)

            def entry(c, s, most):
                return sp.value_load(table[0:1, c, bass.ds(s.n, 1)], min_val=0, max_val=most)

            def of_expert(s, of):
                return of[bass.ds(entry(1, s, NE - 1), 1)] if s.routed else of[NE:NE + 1]

            def step(at):
                s = at(3)
                if s.valid():
                    if s.routed:
                        src = xs_rows[bass.ds(entry(0, s, NE * CAP - TS), TS), :]
                    if s.since(2):
                        sp.wait_ge(d_xs, 2 * (s.n - 2) + 2)
                    if s.routed:
                        sp.dma_start(xr[:, s.par], src.rearrange("(p g) d -> p g d", g=GROUPS))\
                            .then_inc(ld_xr[s.par], 16)
                    else:
                        sp.dma_start(xr[0:SR, s.par], s.tokens(xf_rows)).then_inc(ld_xr[s.par], 16)
                if s.valid() and s.weights():
                    of = of_expert(s, a["w1"])
                    if s.since(1):
                        sp.wait_ge(w1_lo, 2 * s.n)
                    sp.dma_start(w1raw[:], of.rearrange("e p c -> p (e c)")).then_inc(ld_w1, 16)
                if s.valid() and not s.routed:
                    if s.since(NSLOT + 2):
                        sp.wait_ge(d_idx, 5 * (s.k - 2) + 5)
                    sp.dma_start(mrow[:, s.par], s.tokens(meta_rows)).then_inc(ld_meta[s.par], 16)
                s = at(2)
                if s.valid() and s.weights():
                    of = of_expert(s, a["w2"])
                    if s.since(1):
                        sp.wait_ge(w2_hi, 2 * s.n)
                        sp.wait_ge(w2_lo, 2 * s.n)
                    sp.dma_start(w2raw[:], of.rearrange("e p c -> p (e c)")).then_inc(ld_w2, 16)
                s = at(3)
                if s.valid() and s.weights():
                    of = of_expert(s, a["b1"])
                    if s.since(2):
                        sp.wait_ge(sb_h, MH * (s.n - 2) + MH)
                    sp.dma_start(b1[:, s.par], of.rearrange("e p c -> p (e c)"))\
                        .then_inc(ld_b1[s.par], 16)
                s = at(0)
                if s.valid() and s.routed:
                    dst = y_rows[bass.ds(s.n * TS, TS), :]
                    sp.wait_ge(d_y, 2 * s.n + 2)
                    sp.dma_start(dst.rearrange("(p g) d -> p g d", g=GROUPS), ysb[:, s.par]).then_inc(st_y[s.par], 16)
                elif s.valid():
                    sp.wait_ge(d_out, 2 * s.k + 2)
                    sp.dma_start(s.tokens(a["out"]), ysb[0:SR, s.par]).then_inc(st_y[s.par], 16)
                s = at(2)
                if s.valid() and s.weights():
                    of = of_expert(s, a["b2"])
                    if s.since(2):
                        sp.wait_ge(d_y, 2 * (s.n - 2) + 2)
                    sp.dma_start(b2[:, s.par], of.rearrange("e p c -> p (e c)"))\
                        .then_inc(ld_b2[s.par], 16)
                if s.valid() and not s.routed:
                    if s.since(NSLOT + 2):
                        sp.wait_ge(d_out, 2 * (s.k - 2) + 2)
                    sp.dma_start(acc[:, s.par], s.tokens(h2_rows)).then_inc(ld_h2[s.par], 16)

            slots(sp, step)
            for i in range(2):
                sp.wait_ge(st_y[i], 16 * NALL // 2)

        def phase2_pe(pe):
            pe.wait_ge(d_route, ROUTE * B // 2)
            pe.wait_ge(sb_xlnT, B)
            pe.matmul(cnt_ps, ones[0:N, :], cmask[:, 0, 0], start=True, stop=True).then_inc(ps_cnt, 1)
            phase1_over(pe)
            pe.wait_ge(init_v, 4)

            def step(at):
                s = at(1)
                if s.valid():
                    pe.wait_ge(sb_T, 3 * s.n + 3)
                    pe.wait_ge(w1_hi, 3 * s.wn + 3)
                    pe.wait_ge(w1_lo, 2 * s.wn + 2)
                    for m in range(MH):
                        if m >= 3:
                            pe.wait_ge(sb_h, MH * s.n + m - 2)
                        elif s.since(1):
                            pe.wait_ge(sb_h, MH * (s.n - 1) + m + 4)
                        for n, (wt, c) in enumerate(((w1h, 2), (w1h, 1), (w1h, 0), (w1l, 1), (w1l, 0))):
                            mm = pe.matmul(banks[m % 3][:, 0:s.cols], wt[:, s.wpar, c * H + m * P:c * H + (m + 1) * P],
                                           xT[:, s.par, c, 0:s.cols], start=n == 0, stop=n == 4)
                        mm.then_inc(ps_h, 1)
                s = at(2)
                if s.valid():
                    pe.wait_ge(d_xs, 2 * s.n + 2)
                    for c in range(3):
                        if s.since(1):
                            pe.wait_ge(sb_T, 3 * (s.n - 1) + c + 1)
                        for g in range(GROUPS):
                            mm = pe.transpose(banks[5 + c][:, g * s.rows:(g + 1) * s.rows].bitcast(F32R),
                                              xsplit[0:s.rows, g, c * P:(c + 1) * P], identr[0:s.rows, 0:s.rows])
                        mm.then_inc(ps_T, 1)
                s = at(0)
                if s.valid():
                    pe.wait_ge(d_h, 2 * MH * s.n + 2 * MH)
                    pe.wait_ge(w2_hi, 2 * s.wn + 2)
                    pe.wait_ge(w2_lo, 2 * s.wn + 2)
                    for g in range(GROUPS):
                        if g % 2 == 0 and s.since(1):
                            pe.wait_ge(d_y, 2 * (s.n - 1) + g // 2 + 1)
                        n = 0
                        for ht, wt in ((hl, w2h), (hh, w2l), (hh, w2h)):
                            for k in range(MH):
                                mm = pe.matmul(banks[3 + g // 2][0:s.rows, (g % 2) * D:(g % 2 + 1) * D],
                                               ht[:, s.par, k, g * s.rows:(g + 1) * s.rows],
                                               wt[:, s.wpar, k * D:(k + 1) * D], start=n == 0, stop=n == 3 * MH - 1)
                                n += 1
                        if g % 2:
                            mm.then_inc(ps_y, 1)

            slots(pe, step)

        def phase2_act(act):
            phase1_over(act)

            def step(at):
                def w1_high(n):
                    s = at(2)
                    if s.valid() and s.weights():
                        if n == 0:
                            act.wait_ge(ld_w1, 16 * s.n + 16)
                            if s.since(2):
                                act.wait_ge(ps_h, MH * (s.n - 2) + MH)
                                act.wait_ge(w1_lo, 2 * (s.n - 2) + 2)
                        act.activation(w1h[:, s.par, n * H:(n + 1) * H], w1raw[:, n * H:(n + 1) * H], ACT.Copy)\
                            .then_inc(w1_hi, 1)

                def w2_high(n):
                    s = at(1)
                    if s.valid() and s.weights():
                        if n == 0:
                            act.wait_ge(ld_w2, 16 * s.n + 16)
                            if s.since(2):
                                act.wait_ge(ps_y, 2 * (s.n - 2) + 2)
                                act.wait_ge(w2_lo, 2 * (s.n - 2) + 2)
                        half = W2C // 2
                        act.activation(w2h[:, s.par, n * half:(n + 1) * half], w2raw[:, n * half:(n + 1) * half],
                                       ACT.Copy).then_inc(w2_hi, 1)

                def relu(m):
                    s = at(1)
                    if s.valid():
                        if m == 0:
                            act.wait_ge(ld_b1[s.wpar], 16 * s.whalf + 16)
                        act.wait_ge(ps_h, MH * s.n + m + 1)
                        if m >= 2:
                            act.wait_ge(d_h, 2 * (MH * s.n + m - 2) + 2)
                        elif s.since(1):
                            act.wait_ge(d_h, 2 * (MH * (s.n - 1) + m + 4) + 2)
                        act.activation(hf[:, m % 2, 0:s.cols], banks[m % 3][:, 0:s.cols], ACT.Relu,
                                       bias=b1[:, s.wpar, m:m + 1]).then_inc(sb_h, 1)

                for m in range(MH):
                    relu(m)
                    if m < 3:
                        w1_high(m)
                    elif m < 5:
                        w2_high(m - 3)
                s = at(2)
                if s.valid():
                    for c in range(3):
                        act.wait_ge(ps_T, 3 * s.n + c + 1)
                        if c == 0 and s.since(2):
                            act.wait_ge(ps_h, MH * (s.n - 2) + MH)
                        act.activation(xT[:, s.par, c, 0:s.cols], banks[5 + c][:, 0:s.cols], ACT.Copy).then_inc(sb_T, 1)
                if s.valid() and not s.routed:
                    act.wait_ge(d_idx, 5 * s.k + 5)
                    act.activation(gate[:, s.par, 1], gate[:, s.par, 0], ACT.Exp).then_inc(a_gate, 1)

            slots(act, step)

        def phase2_pool(pool):
            phase1_over(pool)

            def step(at):
                def low(s, done, high, highs, raw, hi, lo, cols):
                    for i in range(2):
                        cut = slice(i * cols, (i + 1) * cols)
                        pool.wait_ge(high, highs * s.n + (highs if i else 1))
                        pool.tensor_tensor(lo[:, s.par, cut], raw[:, cut], hi[:, s.par, cut].bitcast(F32),
                                           ALU.subtract).then_inc(done, 1)

                s = at(2)
                if s.valid() and s.weights():
                    if s.since(2):
                        pool.wait_ge(ps_h, MH * (s.n - 2) + MH)
                    low(s, w1_lo, w1_hi, 3, w1raw, w1h, w1l, H)
                s = at(1)
                if s.valid() and s.weights():
                    if s.since(2):
                        pool.wait_ge(ps_y, 2 * (s.n - 2) + 2)
                    low(s, w2_lo, w2_hi, 2, w2raw, w2h, w2l, W2C // 2)
                s = at(0)
                if s.valid() and not s.routed:
                    if not s.since(NSLOT + 1):
                        for i in range(2):
                            pool.wait_ge(st_y[i], 16 * NSLOT // 2)
                    pool.wait_ge(d_idx, 5 * s.k + 4)
                    if s.since(NSLOT + 2):
                        pool.wait_ge(d_acc, 8 * (s.k - 2) + 8)
                    pool.sem_inc(pool_passed, 1)
                    for k in range(2):
                        for g in range(GROUPS):
                            pool.indirect_dma_start(
                                out=ye[:, s.par, k, g], out_offset=None, in_=y_rows,
                                in_offset=bass.IndirectOffsetOnAxis(ap=gidx[:, s.par, g, k:k + 1], axis=0))\
                                .then_inc(gath[s.par], 16)

            slots(pool, step)

        def phase2_dve(dve):
            dve.tensor_copy(identr[:], ident).then_inc(init_v, 1)
            done = [0]

            def chain(ins):
                ins.then_inc(d_tab, 1)
                done[0] += 1
                dve.wait_ge(d_tab, done[0])

            slot_no = consts[0:1, C_SLOT:C_SLOT + NSLOT]
            dve.wait_ge(ps_cnt, 1)
            chain(dve.tensor_copy(cnt[:], cnt_ps))
            chain(dve.tensor_tensor(zrow[:], cnt[0:1, :], consts[0:1, C_CAP:C_CAP + NE], ALU.add))
            chain(dve.tensor_tensor(tcmp[:], cnt[:].unsqueeze(2).broadcast_to([P, NE, NTHR]),
                                    consts[:, C_THR:C_THR + NTHR].unsqueeze(1).broadcast_to([P, NE, NTHR]), ALU.is_gt))
            chain(dve.tensor_reduce(nsl[:], tcmp[:], AX, ALU.add))
            chain(dve.tensor_tensor(tcum[:], consts[0:1, C_LE:C_BIAS].rearrange("p (e f) -> p e f", e=NE),
                                    nsl[0:1].unsqueeze(1).broadcast_to([1, NE, NE]), ALU.mult))
            chain(dve.tensor_reduce(cum[:], tcum[:], AX, ALU.add))
            chain(dve.tensor_scalar(step8[:], nsl[:], -float(TS), float(CAP), ALU.mult, ALU.add))
            chain(dve.tensor_tensor(past[:], slot_no.unsqueeze(2).broadcast_to([1, NSLOT, NE]),
                                    cum[:].unsqueeze(1).broadcast_to([1, NSLOT, NE]), ALU.is_ge))
            chain(dve.tensor_tensor(tmul[:], past[:], step8[0:1].unsqueeze(1).broadcast_to([1, NSLOT, NE]), ALU.mult))
            chain(dve.tensor_reduce(tsum[:, 0], tmul[:, :, 0:NE - 1], AX, ALU.add))
            chain(dve.scalar_tensor_tensor(out=tsum[:, 1], in0=slot_no, scalar=float(TS), in1=tsum[:, 0],
                                           op0=ALU.mult, op1=ALU.add))
            chain(dve.tensor_scalar(tsum[:, 2], past[:, :, NE - 1], -1.0, 1.0, ALU.mult, ALU.add))
            chain(dve.tensor_tensor(tsum[:, 3], tsum[:, 1], tsum[:, 2], ALU.mult))
            chain(dve.tensor_reduce(tsum[:, 4], past[:, :, 0:NE - 1], AX, ALU.add))
            chain(dve.tensor_copy(table[:, 0], tsum[:, 3]))
            chain(dve.tensor_copy(table[:, 1], tsum[:, 4]))
            assert done[0] == TAB
            phase1_over(dve)

            def step(at):
                def split_h(m):
                    s = at(1)
                    if s.valid():
                        base = 2 * (MH * s.n + m)
                        if m == 0 and s.since(2):
                            dve.wait_ge(ps_y, 2 * (s.n - 2) + 2)
                        dve.wait_ge(sb_h, MH * s.n + m + 1)
                        dve.tensor_copy(hh[:, s.par, m, 0:s.cols], hf[:, m % 2, 0:s.cols]).then_inc(d_h, 1)
                        dve.wait_ge(d_h, base + 1)
                        dve.tensor_tensor(hl[:, s.par, m, 0:s.cols], hf[:, m % 2, 0:s.cols],
                                          hh[:, s.par, m, 0:s.cols].bitcast(F32), ALU.subtract).then_inc(d_h, 1)

                split_h(0)
                split_h(1)
                s = at(2)
                if s.valid():
                    dve.wait_ge(ld_xr[s.par], 16 * s.half + 16)
                    if s.since(1):
                        dve.wait_ge(ps_T, 3 * (s.n - 1) + 3)
                    dve.tensor_copy(xsplit[:, :, 0:D], xr[:, s.par]).then_inc(d_xs, 1)
                    dve.wait_ge(d_xs, 2 * s.n + 1)
                    dve.tensor_tensor(xsplit[:, :, D:2 * D], xr[:, s.par], xsplit[:, :, 0:D].bitcast(F32),
                                      ALU.subtract).then_inc(d_xs, 1)
                for m in range(2, MH):
                    split_h(m)
                s = at(1)
                if s.valid() and not s.routed:
                    base = 3 * s.k
                    dve.wait_ge(a_gate, s.k + 1)
                    dve.tensor_scalar(gate[:, s.par, 2], gate[:, s.par, 1], 1.0, None, ALU.add).then_inc(d_gate, 1)
                    dve.wait_ge(d_gate, base + 1)
                    dve.reciprocal(gate[:, s.par, 3], gate[:, s.par, 2]).then_inc(d_gate, 1)
                    dve.wait_ge(d_gate, base + 2)
                    dve.tensor_tensor(gate[:, s.par, 4], gate[:, s.par, 1], gate[:, s.par, 3], ALU.mult)\
                        .then_inc(d_gate, 1)
                s = at(0)
                if s.valid() and not s.routed:
                    base = 8 * s.k
                    dve.wait_ge(d_gate, 3 * s.k + 3)
                    dve.wait_ge(ld_h2[s.par], 16 * s.khalf + 16)
                    dve.wait_ge(gath[s.par], 128 * s.khalf + 128)
                    for k in range(2):
                        for g in range(GROUPS):
                            if k:
                                dve.wait_ge(d_acc, base + g + 1)
                            dve.scalar_tensor_tensor(out=acc[:, s.par, g], in0=ye[:, s.par, k, g],
                                                     scalar=gate[:, s.par, 3 + k, g:g + 1], in1=acc[:, s.par, g],
                                                     op0=ALU.mult, op1=ALU.add).then_inc(d_acc, 1)
                s = at(2)
                if s.valid() and not s.routed:
                    dve.wait_ge(ld_meta[s.par], 16 * s.khalf + 16)
                    base, regions = 5 * s.k, NE - 1
                    shape = [SR, GROUPS, 2, regions]
                    dve.tensor_tensor(behind[:], mrow[:, s.par, :, 2:4].unsqueeze(3).broadcast_to(shape),
                                      consts[0:SR, C_CAP + 1:C_CAP + NE].unsqueeze(1).unsqueeze(1).broadcast_to(shape),
                                      ALU.is_ge).then_inc(d_idx, 1)
                    dve.wait_ge(d_idx, base + 1)
                    dve.tensor_tensor(behind[:], behind[:],
                                      step8[0:SR, 0:regions].unsqueeze(1).unsqueeze(1).broadcast_to(shape),
                                      ALU.mult).then_inc(d_idx, 1)
                    dve.wait_ge(d_idx, base + 2)
                    dve.tensor_reduce(moved[:], behind[:], AX, ALU.add).then_inc(d_idx, 1)
                    dve.wait_ge(d_idx, base + 3)
                    dve.tensor_tensor(gidx[:, s.par], mrow[:, s.par, :, 2:4], moved[:], ALU.subtract).then_inc(d_idx, 1)
                    dve.tensor_tensor(gate[:, s.par, 0], mrow[:, s.par, :, 1], mrow[:, s.par, :, 0],
                                      ALU.subtract).then_inc(d_idx, 1)
                s = at(0)
                if s.valid():
                    dve.wait_ge(ld_b2[s.wpar], 16 * s.whalf + 16)
                    if s.since(2):
                        dve.wait_ge(st_y[s.par], 16 * s.half)
                    r = P if s.routed else SR
                    for j in range(2):
                        dve.wait_ge(ps_y, 2 * s.n + j + 1)
                        dve.tensor_tensor(ysb[0:r, s.par, 2 * j:2 * j + 2],
                                          banks[3 + j][0:r, 0:2 * D].rearrange("p (g d) -> p g d", g=2),
                                          b2[0:r, s.wpar].unsqueeze(1).broadcast_to([r, 2, D]), ALU.add)\
                            .then_inc(d_y, 1)
                if s.valid() and not s.routed:
                    dve.wait_ge(d_acc, 8 * s.k + 8)
                    for j in range(2):
                        dve.wait_ge(d_y, 2 * s.n + j + 1)
                        y = ysb[0:SR, s.par, 2 * j:2 * j + 2]
                        dve.scalar_tensor_tensor(out=y, in0=y, scalar=MOE_SCALE, in1=acc[:, s.par, 2 * j:2 * j + 2],
                                                 op0=ALU.mult, op1=ALU.add).then_inc(d_out, 1)

            slots(dve, step)

        block = ctx.enter_context(nc.Block())

        def quads(eng, step):
            for q in (-1, 0, 1):
                for u in range(4):
                    if 4 * q + u >= -4:
                        step(lambda d, q=q, u=u: Image(q, u + d), u)
            with eng.Fori(2, 15) as q:
                for u in range(4):
                    step(lambda d, q=q, u=u: Image(q, u + d, 2), u)
            for q in (15, 16):
                for u in range(4):
                    step(lambda d, q=q, u=u: Image(q, u + d), u)

        NW1 = 7

        @block.sync
        def _(sp):
            for to, of in ((we, a["we"]), (wqkv, a["wqkv"]), (wo, a["wo"]), (wr, a["wr"]), (gains, a["gains"]),
                           (posb, a["posb"]), (consts, a["consts"])):
                sp.dma_start(to[:], of).then_inc(ld_w, 16)

            def step(at, u):
                b = at(4)
                if b.valid():
                    if b.since(2):
                        sp.wait_ge(ps_emb, b.n - 1)
                    sp.dma_start(xin[:, b.m2], a["x"][bass.ds(b.n, 1)].rearrange("o p k n -> p (o k) n"))\
                        .then_inc(ld_x[b.m2], 16)
                b = at(-2)
                if b.valid():
                    sp.wait_ge(d_ln2, LN2 * b.n + 1)
                    sp.dma_start(h2_rows[bass.ds(b.n * N, N), :], h2[:, b.m2]).then_inc(st_h2[b.m2], 16)
                    sp.wait_ge(d_ln2, LN2 * b.n + LN2)
                    sp.dma_start(xf_rows[bass.ds(b.n * N, N), :], xf[:, b.m4]).then_inc(st_xf[b.m4], 16)
                b = at(-4)
                if b.valid() and u % 2 == 0:
                    sp.wait_ge(d_route, ROUTE * b.half + ROUTE)
                    sp.dma_start(meta_rows[bass.ds(b.n * N, 2 * N), :].rearrange("(j p) c -> p j c", j=2),
                                 meta[:, b.pair]).then_inc(st_meta[b.pair], 16)

            quads(sp, step)
            phase2_sp(sp)

        @block.tensor
        def _(pe):
            def transposes(out, of, width, n):
                for t in range(n):
                    last = pe.transpose(out[0:width, t * N:(t + 1) * N], of[:, t * width:(t + 1) * width],
                                        ident[0:N, 0:N])
                return last

            pe.wait_ge(ld_w, 16 * NW1)
            pe.wait_ge(init_v, 1)
            pe.wait_ge(init_p, 7)

            def step(at, u):
                b = at(0)
                if b.valid():
                    pe.wait_ge(d_qk, QKN * b.n + QKN)
                    transposes(banks[4], qpad[:, b.m2].rearrange("p h c -> p (h c)"), P, NG).then_inc(ps_q, 1)
                    pe.wait_ge(sb_v, b.n + 1)
                    transposes(banks[5], kpad[:, b.m2].rearrange("p h c -> p (h c)"), P, NG).then_inc(ps_k, 1)
                b = at(-2)
                if b.valid():
                    pe.wait_ge(sb_oT, b.n + 1)
                    if b.since(1):
                        pe.wait_ge(d_lg, b.n)
                    for t in range(NG):
                        mm = pe.matmul(wo_ps, oT[:, b.m2, t, :], wo[:, t, :], start=t == 0, stop=t == NG - 1)
                    mm.then_inc(ps_wo, 1)
                b = at(2)
                if b.valid():
                    if b.since(1):
                        pe.wait_ge(sb_xlnT, b.n)
                    pe.wait_ge(ld_x[b.m2], 16 * b.half + 16)
                    for k in range(KE):
                        mm = pe.matmul(emb_ps, xin[:, b.m2, k, :], we[:, k, :], start=k == 0, stop=k == KE - 1)
                    mm.then_inc(ps_emb, 1)
                b = at(0)
                if b.valid():
                    pe.wait_ge(sb_q, NG * b.n + NG)
                    pe.wait_ge(sb_k, b.n + 1)
                    if b.since(2):
                        pe.wait_ge(sb_oT, b.n - 1)
                    for r in range(4):
                        if b.since(1):
                            pe.wait_ge(exps, NH * (b.n - 1) + NG * (r + 1))
                        for t in range(NG):
                            mm = pe.matmul(banks[r][0:N, t * N:(t + 1) * N], kT[32 * r:32 * r + HD, b.m2, t, :],
                                           qT[32 * r:32 * r + HD, b.m2, t, :], start=True, stop=True)
                        mm.then_inc(ps_sc, 1)
                b = at(-4)
                if b.valid() and u % 2 == 0:
                    if at(-2).valid():
                        pe.wait_ge(d_ln2, LN2 * at(-2).n + 1)
                    else:
                        pe.wait_ge(d_lg, B)
                    pe.wait_ge(d_route, ROUTE * b.half + 10)
                    pe.matmul(pre_ps, ones[0:N, 0:N], cmask[:, b.pair].rearrange("p j e -> p (j e)"), start=True, stop=False)
                    pe.matmul(pre_ps, tri, mask[:, b.pair].rearrange("p j e -> p (j e)"), start=False, stop=True)\
                        .then_inc(ps_pre, 1)
                b = at(1)
                if b.valid():
                    pe.wait_ge(sb_xlnT, b.n + 1)
                    if b.since(1):
                        pe.wait_ge(sb_q, NG * b.n)
                    for t in range(2):
                        mm = pe.matmul(banks[4][0:N, 0:2 * D], xlnT[:, b.m2, t, :], wqkv[:, t, 0:2 * D],
                                       start=t == 0, stop=t == 1)
                    mm.then_inc(ps_qk, 1)
                    if b.since(1):
                        pe.wait_ge(sb_k, b.n)
                    for t in range(2):
                        mm = pe.matmul(v_ps, xlnT[:, b.m2, t, :], wqkv[:, t, 2 * D:3 * D],
                                       start=t == 0, stop=t == 1)
                    mm.then_inc(ps_v, 1)
                b = at(2)
                if b.valid():
                    pe.wait_ge(d_ln1, LN1 * b.n + LN1)
                    transposes(banks[7], xln[:, b.m2], DH, 2).then_inc(ps_xlnT, 1)
                b = at(-2)
                if b.valid():
                    pe.wait_ge(d_ln2, LN2 * b.n + LN2)
                    if u % 2 == 0 and b.since(2):
                        pe.wait_ge(d_route, ROUTE * at(-4).half + 11)
                    transposes(banks[6], xf[:, b.m4], DH, 2).then_inc(ps_xfT, 1)
                b = at(-1)
                if b.valid():
                    pe.wait_ge(d_v, 2 * b.n + 2)
                    if at(0).valid():
                        pe.wait_ge(exps, NH * (b.n + 1) + NG)
                    else:
                        pe.wait_ge(exps, NH * b.n + NH)
                        pe.wait_ge(sb_oT, b.n)
                    for hd in range(NH):
                        r, t = hd % 4, hd // 4
                        mm = pe.matmul(banks[0][32 * r:32 * (r + 1), t * N:(t + 1) * N], vn[:, b.m2, hd, :],
                                       probs[:, b.m2, hd, :], start=True, stop=True)
                    mm.then_inc(ps_av, 1)
                b = at(-2)
                if b.valid():
                    pe.wait_ge(sb_xfT, b.n + 1)
                    for t in range(2):
                        mm = pe.matmul(lg_ps, xfT[:, b.m2, t, :], wr[:, t, :], start=t == 0, stop=t == 1)
                    mm.then_inc(ps_lg, 1)

            quads(pe, step)
            phase2_pe(pe)

        @block.scalar
        def _(act):
            def copy(out, ps):
                return act.activation(out, ps, ACT.Copy)

            act.wait_ge(init_v, 1)
            act.wait_ge(init_p, 7)

            def step(at, u):
                b = at(0)
                if b.valid():
                    act.wait_ge(ps_q, b.n + 1)
                    if b.since(2):
                        act.wait_ge(ps_sc, 4 * (b.n - 2) + 4)
                    for t in range(NG):
                        act.activation(qT[:, b.m2, t, :], banks[4][:, t * N:(t + 1) * N], ACT.Copy,
                                       scale=gain[:, t:t + 1]).then_inc(sb_q, 1)
                    act.wait_ge(ps_k, b.n + 1)
                    copy(kT[:, b.m2].rearrange("p t n -> p (t n)"), banks[5][:, 0:NG * N]).then_inc(sb_k, 1)
                    for r in range(4):
                        act.wait_ge(d_max, 4 * b.n + r + 1)
                        if r == 0 and b.since(2):
                            act.wait_ge(ps_av, b.n - 1)
                            act.wait_ge(d_v, 2 * (b.n - 2) + 1)
                        for t in range(NG):
                            hd = 4 * t + r
                            act.activation(probs[:, b.m2, hd, :], banks[r][0:N, t * N:(t + 1) * N], ACT.Exp,
                                           bias=negmax[:, b.m2, hd:hd + 1], accum_out=rowsum[:, b.m2, hd:hd + 1])\
                                .then_inc(exps, 1)
                b = at(1)
                if b.valid():
                    act.wait_ge(ps_v, b.n + 1)
                    if b.since(2):
                        act.wait_ge(d_v, 2 * (b.n - 2) + 2)
                    copy(vsb[:, b.m2], v_ps).then_inc(sb_v, 1)
                b = at(2)
                if b.valid():
                    act.wait_ge(ps_xlnT, b.n + 1)
                    if b.since(2):
                        act.wait_ge(ps_v, b.n - 1)
                    copy(xlnT[0:DH, b.m2].rearrange("p t n -> p (t n)"), banks[7][0:DH, 0:2 * N]).then_inc(sb_xlnT, 1)
                b = at(-2)
                if b.valid():
                    act.wait_ge(ps_xfT, b.n + 1)
                    if b.since(2):
                        act.wait_ge(ps_lg, b.n - 1)
                    copy(xfT[:, b.m2].rearrange("p t n -> p (t n)"), banks[6][0:DH, 0:2 * N]).then_inc(sb_xfT, 1)
                b = at(-1)
                if b.valid():
                    act.wait_ge(ps_av, b.n + 1)
                    if b.since(2):
                        act.wait_ge(ps_wo, b.n - 1)
                    act.activation(oT[:, b.m2].rearrange("p t n -> p (t n)"), banks[0][:, 0:NG * N], ACT.Identity,
                                   bias=consts[:, C_BIAS:C_BIAS + 1]).then_inc(sb_oT, 1)

            quads(act, step)
            phase2_act(act)

        @block.gpsimd
        def _(pool):
            pool.memset(ones[:], 1.0).then_inc(init_p, 1)
            pool.memset(qpad[:], 0.0).then_inc(init_p, 1)
            pool.memset(kpad[:], 0.0).then_inc(init_p, 1)
            pool.wait_ge(init_p, 3)
            pool.memset(xlnT[DH:DH + 1], 1.0).then_inc(init_p, 1)
            pool.wait_ge(init_p, 4)
            pool.memset(vn[:], 0.0).then_inc(init_p, 1)
            pool.wait_ge(init_p, 5)
            pool.memset(mhalf[:], -0.5).then_inc(init_p, 1)
            pool.memset(ztile[:], 0.0).then_inc(init_p, 1)
            pool.wait_ge(init_p, 7)

            def step(at, u):
                b = at(-2)
                if b.valid():
                    pool.wait_ge(d_ln2, LN2 * b.n + 4)
                    pool.tensor_tensor(rs2[:, b.m2], ve2[:, b.m2], mhalf[:, 0:1], ALU.pow).then_inc(p_rs2, 1)
                b = at(2)
                if b.valid():
                    pool.wait_ge(d_ln1, LN1 * b.n + 4)
                    if b.since(2):
                        pool.wait_ge(d_ln1, LN1 * (b.n - 2) + 5)
                    pool.tensor_tensor(rs1[:, b.m2], ve1[:, b.m2], mhalf[:, 0:1], ALU.pow).then_inc(p_rs1, 1)
                b = at(1)
                if b.valid():
                    pool.wait_ge(d_qk, QKN * b.n + 5)
                    pool.tensor_tensor(rsq[:, b.m2], veq[:, b.m2], mhalf[:], ALU.pow).then_inc(p_rsq, 1)
                b = at(2)
                if b.valid():
                    pool.wait_ge(d_ln1, LN1 * b.n + LN1)
                    if b.since(4):
                        pool.wait_ge(d_ln2, LN2 * (b.n - 4) + 1)
                    pool.tensor_tensor(hx[:, b.m4], h[:, b.m2], xln[:, b.m2], ALU.add).then_inc(p_hx, 1)
                b = at(-4)
                if b.valid():
                    pool.wait_ge(d_route, ROUTE * b.half + ROUTE)
                    pool.sem_inc(pool_passed, 1)
                    for k in range(2):
                        pool.indirect_dma_start(
                            out=xs_rows,
                            out_offset=bass.IndirectOffsetOnAxis(ap=dest[:, b.pair, b.m2, k:k + 1], axis=0),
                            in_=xf[:, b.m4], in_offset=None).then_inc(scat[b.m4], 16)

            quads(pool, step)
            phase2_pool(pool)

        @block.vector
        def _(dve):
            dve.wait_ge(ld_w, 16 * NW1)
            dve.scalar_tensor_tensor(out=gain[:], in0=gains[:, 0], scalar=HSCALE, in1=gains[:, 1],
                                     op0=ALU.mult, op1=ALU.mult).then_inc(init_v, 1)
            dve.tensor_tensor(posb[:, 0], posb[:, 0], posb[:, 1], ALU.add).then_inc(init_v, 1)
            dve.memset(cmask[:, 0, 0], 0.0).then_inc(init_v, 1)
            dve.wait_ge(init_v, 3)
            dve.wait_ge(init_p, 7)

            def norm_stats(b, src, s, mv, ve, done, base):
                dve.bn_stats(s, src).then_inc(done, 1)
                dve.wait_ge(done, base + 1)
                dve.sem_inc(dve_passed, 1)
                dve.bn_aggr(mv, s).then_inc(done, 1)
                dve.wait_ge(done, base + 2)
                dve.tensor_scalar(ve, mv[:, 1:2], EPS, None, ALU.add).then_inc(done, 1)

            def step(at, u):
                def maxima(r):
                    b = at(0)
                    if not b.valid():
                        return
                    dve.wait_ge(ps_sc, 4 * b.n + r + 1)
                    if r == 0 and b.since(2):
                        dve.wait_ge(exps, NH * (b.n - 2) + NH)
                    dve.tensor_reduce(negmax[:, b.m2, r:NH:4],
                                      banks[r][0:N, 0:NG * N].rearrange("p (t n) -> p t n", t=NG),
                                      AX, ALU.max, negate=True).then_inc(d_max, 1)

                b = at(-1)
                if b.valid():
                    dve.wait_ge(exps, NH * b.n + NH)
                    dve.reciprocal(rinv[:, b.m2], rowsum[:, b.m2]).then_inc(d_v, 1)
                    dve.wait_ge(d_v, 2 * b.n + 1)
                    dve.wait_ge(sb_v, b.n + 1)
                    if b.since(2):
                        dve.wait_ge(ps_av, b.n - 1)
                    dve.tensor_tensor(vn[:, b.m2, :, 0:HD],
                                      vsb[:, b.m2].rearrange("p (h c) -> p h c", h=NH),
                                      rinv[:, b.m2].unsqueeze(2).broadcast_to([N, NH, HD]), ALU.mult).then_inc(d_v, 1)
                b = at(-2)
                if b.valid():
                    dve.wait_ge(ps_wo, b.n + 1)
                    dve.wait_ge(p_hx, b.n + 1)
                    if b.since(2):
                        dve.wait_ge(st_h2[b.m2], 16 * b.half)
                    dve.tensor_tensor(h2[:, b.m2], wo_ps, hx[:, b.m4], ALU.add).then_inc(d_ln2, 1)
                    dve.wait_ge(d_ln2, LN2 * b.n + 1)
                    if b.since(2):
                        dve.wait_ge(p_rs2, b.n - 1)
                    norm_stats(b, h2[:, b.m2], st2[:, b.m2], mv2[:, b.m2], ve2[:, b.m2], d_ln2, LN2 * b.n + 1)
                b = at(2)
                if b.valid():
                    dve.wait_ge(ps_emb, b.n + 1)
                    if b.since(2):
                        dve.wait_ge(p_hx, b.n - 1)
                    dve.tensor_tensor(h[:, b.m2], emb_ps, posb[:, 0], ALU.add).then_inc(d_ln1, 1)
                    dve.wait_ge(d_ln1, LN1 * b.n + 1)
                    norm_stats(b, h[:, b.m2], st1[:, b.m2], mv1[:, b.m2], ve1[:, b.m2], d_ln1, LN1 * b.n + 1)
                maxima(0)
                b = at(-2)
                if b.valid():
                    dve.wait_ge(p_rs2, b.n + 1)
                    if b.since(4):
                        dve.wait_ge(st_xf[b.m4], 16 * b.quad)
                        dve.wait_ge(scat[b.m4], 32 * b.quad)
                        dve.wait_ge(ps_xfT, b.n - 3)
                    dve.tensor_scalar(xf[:, b.m4], h2[:, b.m2], mv2[:, b.m2, 0:1], rs2[:, b.m2],
                                      ALU.subtract, ALU.mult).then_inc(d_ln2, 1)
                maxima(1)
                b = at(2)
                if b.valid():
                    dve.wait_ge(p_rs1, b.n + 1)
                    if b.since(2):
                        dve.wait_ge(ps_xlnT, b.n - 1)
                    dve.tensor_scalar(xln[:, b.m2], h[:, b.m2], mv1[:, b.m2, 0:1], rs1[:, b.m2],
                                      ALU.subtract, ALU.mult).then_inc(d_ln1, 1)
                maxima(2)
                maxima(3)
                b = at(-4)
                if b.valid() and u % 2 == 0:
                    pp, base = b.pair, ROUTE * b.half
                    dve.wait_ge(ps_pre, b.half + 1)
                    dve.tensor_tensor(place[:, pp], pre_ps.rearrange("p (j e) -> p j e", j=2),
                                      consts[0:N, C_CAP:C_CAP + NE].unsqueeze(1).broadcast_to([N, 2, NE]),
                                      ALU.add).then_inc(d_route, 1)
                    dve.wait_ge(d_route, base + 11)
                    for j in range(2):
                        dve.tensor_tensor(picked[:, pp, j], hot[:, pp, j],
                                          place[:, pp, j].unsqueeze(1).broadcast_to([N, 2, NE]), ALU.mult)\
                            .then_inc(d_route, 1)
                    dve.wait_ge(d_route, base + 13)
                    if b.since(4):
                        dve.wait_ge(st_meta[pp], 16 * (b.quad))
                        dve.wait_ge(scat[b.m4], 32 * (b.quad))
                        dve.wait_ge(scat[b.m4 + 1], 32 * (b.quad))
                    dve.tensor_reduce(meta[:, pp, :, 2:4], picked[:, pp], AX, ALU.add).then_inc(d_route, 1)
                    dve.wait_ge(d_route, base + 14)
                    dve.tensor_copy(dest[:, pp], meta[:, pp, :, 2:4]).then_inc(d_route, 1)
                b = at(1)
                if b.valid():
                    dve.wait_ge(ps_qk, b.n + 1)
                    for j in range(2):
                        dve.bn_stats(stq[:, b.m2, j], banks[4][0:N, j * D:(j + 1) * D]).then_inc(d_qk, 1)
                    dve.wait_ge(d_qk, QKN * b.n + 2)
                    dve.sem_inc(dve_passed, 1)
                    for j in range(2):
                        dve.bn_aggr(mvq[:, b.m2, j], stq[:, b.m2, j]).then_inc(d_qk, 1)
                    dve.wait_ge(d_qk, QKN * b.n + 4)
                    if b.since(2):
                        dve.wait_ge(p_rsq, b.n - 1)
                    dve.tensor_scalar(veq[:, b.m2], mvq[:, b.m2, :, 1], EPS, None, ALU.add).then_inc(d_qk, 1)
                b = at(1)
                if b.valid():
                    dve.wait_ge(p_rsq, b.n + 1)
                    if b.since(2):
                        dve.wait_ge(ps_k, b.n - 1)
                    for j, pad in enumerate((qpad, kpad)):
                        dve.tensor_scalar(pad[:, b.m2, :, 0:HD],
                                          banks[4][0:N, j * D:(j + 1) * D].rearrange("p (h c) -> p h c", h=NH),
                                          mvq[:, b.m2, j, 0:1], rsq[:, b.m2, j:j + 1],
                                          ALU.subtract, ALU.mult).then_inc(d_qk, 1)
                b = at(-2)
                if b.valid():
                    dve.wait_ge(ps_lg, b.n + 1)
                    dve.tensor_copy(lg[:, b.pair, b.m2], lg_ps).then_inc(d_lg, 1)
                if b.valid() and u % 2 == 1:
                    pp, base = b.pair, ROUTE * b.half
                    dve.wait_ge(d_lg, b.n + 1)
                    dve.sem_inc(dve_passed, 1)
                    for j in range(2):
                        dve.max(top[:, pp, j], lg[:, pp, j]).then_inc(d_route, 1)
                    dve.wait_ge(d_route, base + 2)
                    dve.sem_inc(dve_passed, 1)
                    for j in range(2):
                        dve.max_index(topi[:, pp, j], top[:, pp, j], lg[:, pp, j]).then_inc(d_route, 1)
                    if b.since(5):
                        dve.wait_ge(st_meta[pp], 16 * (b.quad))
                    dve.tensor_copy(meta[:, pp, :, 0:2], top[:, pp, :, 0:2]).then_inc(d_route, 1)
                    dve.wait_ge(d_route, base + 4)
                    for j in range(2):
                        dve.tensor_tensor(hot[:, pp, j],
                                          consts[0:N, C_IOTA:C_IOTA + NE].unsqueeze(1).broadcast_to([N, 2, NE]),
                                          topi[:, pp, j, 0:2].unsqueeze(2).broadcast_to([N, 2, NE]),
                                          ALU.is_equal).then_inc(d_route, 1)
                    dve.wait_ge(d_route, base + 7)
                    dve.tensor_tensor(mask[:, pp], hot[:, pp, :, 0], hot[:, pp, :, 1], ALU.add).then_inc(d_route, 1)
                    dve.wait_ge(d_route, base + 8)
                    dve.tensor_tensor(cmask[:, pp, 1], cmask[:, pp, 0], mask[:, pp, 0], ALU.add).then_inc(d_route, 1)
                    dve.wait_ge(d_route, base + 9)
                    dve.tensor_tensor(cmask[:, 1 - pp, 0], cmask[:, pp, 1], mask[:, pp, 1], ALU.add)\
                        .then_inc(d_route, 1)

            quads(dve, step)
            phase2_dve(dve)


def kernel(**inputs):
    import numpy as np
    import concourse.bacc as bacc
    from concourse.bass_utils import run_bass_kernel_spmd

    def f(name):
        return np.asarray(inputs[name])

    x = np.pad(f("x"), ((0, 0), (0, 0), (3, 3), (3, 3))).reshape(B, 4, 11, 13, 11, 13)
    x = x.transpose(0, 1, 3, 5, 2, 4).reshape(B, 676, N)
    x = np.pad(x, ((0, 0), (0, KE * P - 676), (0, 0))).reshape(B, KE, P, N).transpose(0, 2, 1, 3)
    we = np.pad(f("L0_tok_W").T, ((0, KE * P - 676), (0, 0))).reshape(KE, P, D).transpose(1, 0, 2)

    def with_bias(weight, bias):
        t = np.zeros((DH + 1, 2, weight.shape[0]), weight.dtype)
        t[0:DH] = weight.T.reshape(2, DH, -1).transpose(1, 0, 2)
        t[DH, 1] = bias
        return t

    wqkv = np.concatenate([with_bias(f("L0_attn_Wq"), np.zeros(D, np.float32)),
                           with_bias(f("L0_attn_Wk"), f("L0_attn_bk")),
                           with_bias(f("L0_attn_Wv"), f("L0_attn_bv"))], axis=2)
    wo = np.zeros((4, 32, NG, D), np.float32)
    wo[:, 0:HD] = f("L0_attn_Wo").T.reshape(NG, 4, HD, D).transpose(1, 2, 0, 3)
    wo[0, HD, 0] = f("L0_attn_bo")
    wo = wo.reshape(P, NG, D)
    wr = f("L0_ffn_Wr").T.reshape(2, DH, NE).transpose(1, 0, 2)
    gains = np.zeros((P, 2, NG), np.float32)
    for j, name in enumerate(("L0_attn_gq", "L0_attn_gk")):
        gains.reshape(4, 32, 2, NG)[:, 0:HD, j] = f(name).reshape(NG, 4, HD).transpose(1, 2, 0)
    posb = np.stack([f("L0_tok_pos_emb"), np.broadcast_to(f("L0_tok_b"), (N, D))], axis=1)

    w1 = np.concatenate([f("L0_ffn_W1"), f("L0_ffn_sW1")[None]]).transpose(0, 2, 1)
    w1 = np.stack([w1[:, 0:P], np.concatenate([w1[:, P:D], w1[:, 0:2 * P - D]], axis=1), w1[:, 2 * P - D:D]], axis=2)
    w2 = np.concatenate([f("L0_ffn_W2"), f("L0_ffn_sW2")[None]]).transpose(0, 2, 1)
    w2 = w2.reshape(NE + 1, MH, P, D).transpose(0, 2, 1, 3)
    b1 = np.concatenate([f("L0_ffn_b1"), f("L0_ffn_sb1")[None]]).reshape(NE + 1, MH, P).transpose(0, 2, 1)
    b2 = np.concatenate([f("L0_ffn_b2"), f("L0_ffn_sb2")[None]])
    b2 = np.broadcast_to(b2[:, None], (NE + 1, P, D))

    consts = np.zeros((P, C_END), np.float32)
    consts[:, C_ID:C_ID + P] = np.eye(P)
    consts[:, C_TRI:C_TRI + P] = np.triu(np.ones((P, P)), 1)
    consts[:, C_IOTA:C_IOTA + NE] = np.arange(NE)
    consts[:, C_CAP:C_CAP + NE] = np.arange(NE) * CAP
    consts[:, C_THR:C_THR + NTHR] = np.arange(NTHR) * TS
    consts[:, C_SLOT:C_SLOT + NSLOT] = np.arange(NSLOT)
    consts[:, C_LE:C_BIAS] = np.tril(np.ones((NE, NE))).reshape(-1)

    consts[HD, C_BIAS] = 1

    arrays = {"x": x, "we": we, "wqkv": wqkv, "wo": wo, "wr": wr,
              "gains": gains, "posb": posb, "w1": w1.reshape(NE + 1, P, W1C), "w2": w2.reshape(NE + 1, P, W2C),
              "b1": b1, "b2": b2, "consts": consts}
    arrays = {f"in_{k}": np.ascontiguousarray(v) for k, v in arrays.items()}

    nc = bacc.Bacc("TRN2", target_bir_lowering=False, num_devices=1)
    a = {k[3:]: nc.dram_tensor(k, v.shape, F32, kind="ExternalInput").ap() for k, v in arrays.items()}
    a["out"] = nc.dram_tensor("out", [T, D], F32, kind="ExternalOutput").ap()
    build(nc, a)
    r = run_bass_kernel_spmd(nc, [arrays], core_ids=[0])
    return np.asarray(r.results[0]["out"]).reshape(B, N, D)
```

```python
from contextlib import ExitStack

import concourse.bass as bass
from concourse import mybir

F32 = mybir.dt.float32
F32R = mybir.dt.float32r
U32 = mybir.dt.uint32
ALU = mybir.AluOpType
ACT = mybir.ActivationFunctionType
AX = mybir.AxisListType.X

P = 128
B = 64
N = 121
T = B * N
D = 192
DH = D // 2
NH = 12
HD = 16
NG = NH // 4
NE = 8
H = 768
MH = H // P
KE = 6
EPS = 1e-5
HSCALE = float(HD) ** -0.5
MOE_SCALE = 0.2

GROUPS = 4
TS = GROUPS * P
CAP = T + TS
NSLOT = (2 * T + NE * (TS - 1)) // TS
NTHR = -(-T // TS)
SH = 16
SR = T // SH // GROUPS
SE = SR + SR % 2
W1C, W2C = 2 * H, MH * D

NALL = NSLOT + SH
assert NSLOT % 2 == 0 and NALL % 2 == 0
TAB = 16

C_ID = 0
C_TRI = C_ID + P
C_IOTA = C_TRI + P
C_CAP = C_IOTA + NE
C_THR = C_CAP + NE
C_SLOT = C_THR + NTHR
C_LE = C_SLOT + NSLOT
C_BIAS = C_LE + NE * NE
C_END = C_BIAS + 1


class Image:

    def __init__(self, q, off, least=None):
        self.q, self.off = q, off
        self.fixed = least is None
        self.least = 4 * (q if self.fixed else least) + off
        self.n = 4 * q + off
        self.m4, self.m2, self.pair = off % 4, off % 2, (off // 2) % 2
        self.quad = q + off // 4
        self.half = 2 * q + off // 2

    def valid(self):
        return not self.fixed or 0 <= self.n < B

    def since(self, k):
        assert self.fixed or self.least >= k
        return self.least >= k


class Slot:

    def __init__(self, q, off, least=None):
        self.fixed = least is None
        self.least = 2 * (q if self.fixed else least) + off
        self.n = 2 * q + off
        self.par = off % 2
        self.half = q + off // 2
        self.routed = self.least < NSLOT
        self.k = self.n - NSLOT
        self.khalf = self.half - NSLOT // 2
        self.wn = self.n if self.routed else NSLOT
        self.wpar = self.par if self.routed else 0
        self.whalf = self.half if self.routed else NSLOT // 2
        self.rows = P if self.routed else SE
        self.cols = GROUPS * self.rows

    def valid(self):
        return not self.fixed or 0 <= self.n < NALL

    def weights(self):
        return self.least <= NSLOT

    def since(self, k):
        assert self.fixed or self.least >= k or not self.routed or k > NSLOT
        return self.least >= k

    def tokens(self, rows):
        return rows[bass.ds(self.k * (SR * GROUPS), SR * GROUPS), :].rearrange("(p g) d -> p g d", g=GROUPS)


def build(nc, a):
    ctx = ExitStack()
    with ctx:
        def sb(name, shape, dt=F32, c=ctx):
            return c.enter_context(nc.sbuf_tensor(name, shape, dt))

        def sem(name):
            return ctx.enter_context(nc.semaphore(name))

        banks = [ctx.enter_context(nc.psum_tensor(f"bank{i}", [P, 512], F32)) for i in range(8)]

        wo_ps, pre_ps, lg_ps = banks[6][0:N, 0:D], banks[6][0:N, 0:2 * NE], banks[7][0:N, 0:NE]
        emb_ps, v_ps = banks[7][0:N, 0:D], banks[5][0:N, 0:D]
        cnt_ps = banks[7][:, 0:NE]

        xs_rows = nc.dram_tensor("xs_rows", [NE * CAP, D], F32, kind="Internal").ap()
        y_rows = nc.dram_tensor("y_rows", [NSLOT * TS, D], F32, kind="Internal").ap()
        xf_rows = nc.dram_tensor("xf_rows", [T, D], F32, kind="Internal").ap()
        h2_rows = nc.dram_tensor("h2_rows", [T, D], F32, kind="Internal").ap()
        meta_rows = nc.dram_tensor("meta_rows", [T, 4], F32, kind="Internal").ap()

        consts = sb("consts", [P, C_END])
        ident = consts[:, C_ID:C_ID + P]
        tri = consts[0:N, C_TRI:C_TRI + N]
        identr = sb("identr", [P, P], F32R)
        ones = sb("ones", [P, P])
        cmask = sb("cmask", [N, 2, 2, NE])
        table = sb("table", [1, 2, NSLOT], U32)
        zrow = sb("zrow", [1, NE], U32)

        w1raw = sb("w1raw", [P, W1C])
        w2raw = sb("w2raw", [P, W2C])
        b1 = sb("b1", [P, 2, MH])
        b2 = sb("b2", [P, 2, D])
        xr = sb("xr", [P, 2, GROUPS, D])
        xsplit = sb("xsplit", [P, GROUPS, 2 * D], F32R)
        xT = sb("xT", [P, 2, 3, TS], F32R)
        hf = sb("hf", [P, 2, TS])
        ysb = sb("ysb", [P, 2, GROUPS, D])

        ztile = sb("ztile", [P, GROUPS * D])
        cnt = sb("cnt", [P, NE])
        tcmp = sb("tcmp", [P, NE, NTHR])
        nsl = sb("nsl", [P, NE])
        tcum = sb("tcum", [1, NE, NE])
        cum = sb("cum", [1, NE])
        step8 = sb("step8", [P, NE])
        past = sb("past", [1, NSLOT, NE])
        tmul = sb("tmul", [1, NSLOT, NE])
        tsum = sb("tsum", [1, 5, NSLOT])

        one = ExitStack()
        we = sb("we", [P, KE, D], F32, one)
        wqkv = sb("wqkv", [DH + 1, 2, 3 * D], F32, one)
        wo = sb("wo", [P, NG, D], F32, one)
        wr = sb("wr", [DH, 2, NE], F32, one)
        gains = sb("gains", [P, 2, NG], F32, one)
        gain = sb("gain", [P, NG], F32, one)
        posb = sb("posb", [N, 2, D], F32, one)
        mhalf = sb("mhalf", [N, 2], F32, one)
        xin = sb("xin", [P, 2, KE, N], F32, one)
        h = sb("h", [N, 2, D], F32, one)
        xln = sb("xln", [N, 2, D], F32, one)
        hx = sb("hx", [N, 4, D], F32, one)
        st1 = sb("st1", [N, 2, 6], F32, one)
        mv1 = sb("mv1", [N, 2, 2], F32, one)
        ve1 = sb("ve1", [N, 2, 1], F32, one)
        rs1 = sb("rs1", [N, 2, 1], F32, one)
        stq = sb("stq", [N, 2, 2, 6], F32, one)
        mvq = sb("mvq", [N, 2, 2, 2], F32, one)
        veq = sb("veq", [N, 2, 2], F32, one)
        rsq = sb("rsq", [N, 2, 2], F32, one)
        st2 = sb("st2", [N, 2, 6], F32, one)
        mv2 = sb("mv2", [N, 2, 2], F32, one)
        ve2 = sb("ve2", [N, 2, 1], F32, one)
        rs2 = sb("rs2", [N, 2, 1], F32, one)
        xlnT = sb("xlnT", [DH + 1, 2, 2, N], F32, one)
        qpad = sb("qpad", [N, 2, NH, 32], F32, one)
        kpad = sb("kpad", [N, 2, NH, 32], F32, one)
        qT = sb("qT", [P, 2, NG, N], F32, one)
        kT = sb("kT", [P, 2, NG, N], F32, one)
        vsb = sb("vsb", [N, 2, D], F32, one)
        vn = sb("vn", [N, 2, NH, 32], F32, one)
        negmax = sb("negmax", [N, 2, NH], F32, one)
        rowsum = sb("rowsum", [N, 2, NH], F32, one)
        rinv = sb("rinv", [N, 2, NH], F32, one)
        probs = sb("probs", [N, 2, NH, N], F32, one)
        oT = sb("oT", [P, 2, NG, N], F32, one)
        h2 = sb("h2", [N, 2, D], F32, one)
        xf = sb("xf", [N, 4, D], F32, one)
        xfT = sb("xfT", [DH, 2, 2, N], F32, one)
        lg = sb("lg", [N, 2, 2, NE], F32, one)
        top = sb("top", [N, 2, 2, NE], F32, one)
        topi = sb("topi", [N, 2, 2, NE], U32, one)
        hot = sb("hot", [N, 2, 2, 2, NE], F32, one)
        mask = sb("mask", [N, 2, 2, NE], F32, one)
        place = sb("place", [N, 2, 2, NE], F32, one)
        picked = sb("picked", [N, 2, 2, 2, NE], F32, one)
        meta = sb("meta", [N, 2, 2, 4], F32, one)
        dest = sb("dest", [N, 2, 2, 2], U32, one)
        one.close()
        w1h = sb("w1h", [P, 2, W1C], F32R)
        w1l = sb("w1l", [P, 2, W1C], F32R)
        w2s = sb("w2s", [P, 2, MH, 2, D], F32R)
        hh = sb("hh", [P, 2, MH, TS], F32R)
        hl = sb("hl", [P, 2, MH, TS], F32R)
        acc = sb("acc", [SR, 2, GROUPS, D])
        b2s = sb("b2s", [SR, D])
        ye = sb("ye", [SR, 2, 2, GROUPS, D])
        mrow = sb("mrow", [SR, 2, GROUPS, 4])
        gidx = sb("gidx", [SR, 2, GROUPS, 2], U32)
        behind = sb("behind", [SR, GROUPS, 2, NE - 1])
        moved = sb("moved", [SR, GROUPS, 2])
        gate = sb("gate", [SR, 2, 5, GROUPS])

        ld_we, ld_w = sem("ld_we"), sem("ld_w")
        ld_x = [sem(f"ld_x{i}") for i in range(2)]
        st_h2 = [sem(f"st_h2{i}") for i in range(2)]
        st_xf = [sem(f"st_xf{i}") for i in range(4)]
        st_meta = [sem(f"st_meta{i}") for i in range(2)]
        scat = [sem(f"scat{i}") for i in range(4)]
        ps_emb, ps_q, ps_k, ps_av, ps_qk, ps_v, ps_sc, ps_xfT, ps_xlnT, ps_wo, ps_lg, ps_pre = (
            sem(n) for n in ("ps_emb", "ps_q", "ps_k", "ps_av", "ps_qk", "ps_v", "ps_sc", "ps_xfT",
                             "ps_xlnT", "ps_wo", "ps_lg", "ps_pre"))
        sb_q, sb_k, sb_v, sb_oT, sb_xfT, sb_xlnT, exps = (
            sem(n) for n in ("sb_q", "sb_k", "sb_v", "sb_oT", "sb_xfT", "sb_xlnT", "exps"))
        d_ln1, d_qk, d_max, d_v, d_ln2, d_lg, d_route = (
            sem(n) for n in ("d_ln1", "d_qk", "d_max", "d_v", "d_ln2", "d_lg", "d_route"))
        p_rs1, p_rsq, p_rs2, p_hx = (sem(n) for n in ("p_rs1", "p_rsq", "p_rs2", "p_hx"))
        dve_passed, pool_passed = sem("dve_passed"), sem("pool_passed")
        init_v, init_p = sem("init_v"), sem("init_p")
        ps_cnt, d_tab, st_zero = sem("ps_cnt"), sem("d_tab"), [sem(f"st_zero{i}") for i in range(2)]
        ld_w1, ld_w2 = sem("ld_w1"), sem("ld_w2")
        ld_b1, ld_b2, ld_xr, ld_meta, ld_h2, st_y = (
            [sem(f"{n}{i}") for i in range(2)] for n in ("ld_b1", "ld_b2", "ld_xr", "ld_meta", "ld_h2", "st_y"))
        gath = [[sem(f"gath{i}{k}") for k in range(2)] for i in range(2)]
        w1_hi, w1_lo, w2_hi, w2_lo = (sem(n) for n in ("w1_hi", "w1_lo", "w2_hi", "w2_lo"))
        d_xs, ps_T, sb_T, ps_h, sb_h, d_h, ps_y, d_y, p_h2 = (
            sem(n) for n in ("d_xs", "ps_T", "sb_T", "ps_h", "sb_h", "d_h", "ps_y", "d_y", "p_h2"))
        p_b2 = sem("p_b2")
        d_idx, a_gate, d_gate, d_acc = (sem(n) for n in ("d_idx", "a_gate", "d_gate", "d_acc"))
        LN1, QKN, LN2, ROUTE = 5, 7, 5, 15

        def phase1_over(eng):
            for i in range(4):
                eng.wait_ge(scat[i], 32 * B // 4)
                eng.wait_ge(st_xf[i], 16 * B // 4)
            for i in range(2):
                eng.wait_ge(st_h2[i], 16 * B // 2)
                eng.wait_ge(st_meta[i], 16 * B // 4)
            eng.wait_ge(exps, NH * B)
            eng.wait_ge(sb_xfT, B)
            eng.wait_ge(ps_cnt, 1)
            eng.wait_ge(d_route, ROUTE * B // 2)
            eng.wait_ge(p_rs2, B)

        def slots(eng, step):
            def straight(q0, q1):
                for q in range(q0, q1):
                    for u in range(2):
                        step(lambda d, q=q, u=u: Slot(q, u + d))

            def loop(q0, q1):
                with eng.Fori(q0, q1) as q:
                    for u in range(2):
                        step(lambda d, q=q, u=u: Slot(q, u + d, q0))

            straight(-2, 1)
            loop(1, NSLOT // 2 - 2)
            straight(NSLOT // 2 - 2, NSLOT // 2 + 1)
            loop(NSLOT // 2 + 1, NALL // 2 - 2)
            straight(NALL // 2 - 2, NALL // 2)

        def zero_rows(eng, experts):
            eng.wait_ge(d_tab, TAB)
            eng.wait_ge(init_p, 7)
            for i in range(4):
                eng.wait_ge(scat[i], 32 * B // 4)
            for e in experts:
                row = eng.value_load(zrow[0:1, e:e + 1], min_val=0, max_val=NE * CAP - TS)
                eng.dma_start(xs_rows[bass.ds(row, TS), :].rearrange("(p g) d -> p (g d)", g=GROUPS), ztile[:])\
                    .then_inc(st_zero[experts[0] % 2], 16)

        def phase2_sp(sp):
            sp.wait_ge(d_tab, TAB)

            def entry(c, s, most):
                return sp.value_load(table[0:1, c, bass.ds(s.n, 1)], min_val=0, max_val=most)

            def of_expert(s, of):
                return of[bass.ds(entry(1, s, NE - 1), 1)] if s.routed else of[NE:NE + 1]

            def step(at):
                s = at(3)
                if s.valid() and s.weights():
                    of = of_expert(s, a["w1"])
                    if s.since(1):
                        sp.wait_ge(w1_lo, 2 * s.n)
                    sp.dma_start(w1raw[:], of.rearrange("e p c -> p (e c)")).then_inc(ld_w1, 16)
                if s.valid():
                    if s.fixed and s.n == 0:
                        zero_rows(sp, range(1, NE, 2))
                        for i in range(2):
                            sp.wait_ge(st_zero[i], 16 * NE // 2)
                        phase1_over(sp)
                    if s.routed:
                        src = xs_rows[bass.ds(entry(0, s, NE * CAP - TS), TS), :]
                    if s.since(2):
                        sp.wait_ge(d_xs, 3 * (s.n - 2) + 3)
                    if s.routed:
                        sp.dma_start(xr[:, s.par], src.rearrange("(p g) d -> p g d", g=GROUPS))\
                            .then_inc(ld_xr[s.par], 16)
                    else:
                        sp.dma_start(xr[0:SR, s.par], s.tokens(xf_rows)).then_inc(ld_xr[s.par], 16)
                if s.valid() and not s.routed:
                    if s.since(NSLOT + 2):
                        sp.wait_ge(d_idx, 5 * (s.k - 2) + 5)
                    sp.dma_start(mrow[:, s.par], s.tokens(meta_rows)).then_inc(ld_meta[s.par], 16)
                s = at(2)
                if s.valid() and s.weights():
                    of = of_expert(s, a["w2"])
                    if s.since(1):
                        sp.wait_ge(w2_hi, 2 * s.n)
                        sp.wait_ge(w2_lo, 2 * s.n)
                    sp.dma_start(w2raw[:], of.rearrange("e p c -> p (e c)")).then_inc(ld_w2, 16)
                s = at(3)
                if s.valid() and s.weights():
                    of = of_expert(s, a["b1"])
                    if s.since(2):
                        sp.wait_ge(sb_h, 2 * MH * (s.n - 1))
                    sp.dma_start(b1[:, s.par], of.rearrange("e p c -> p (e c)"))\
                        .then_inc(ld_b1[s.par], 16)
                s = at(0)
                if s.valid() and s.routed:
                    dst = y_rows[bass.ds(s.n * TS, TS), :]
                    sp.wait_ge(d_y, 2 * GROUPS * (s.n + 1))
                    sp.dma_start(dst.rearrange("(p g) d -> p g d", g=GROUPS), ysb[:, s.par]).then_inc(st_y[s.par], 16)
                elif s.valid():
                    sp.wait_ge(d_acc, 8 * s.k + 8)
                    sp.dma_start(s.tokens(a["out"]), ysb[0:SR, s.par]).then_inc(st_y[s.par], 16)
                s = at(2)
                if s.valid() and s.weights():
                    of = of_expert(s, a["b2"])
                    if s.since(2):
                        sp.wait_ge(d_y, 2 * GROUPS * (s.n - 1))
                    sp.dma_start(b2[:, s.par], of.rearrange("e p c -> p (e c)"))\
                        .then_inc(ld_b2[s.par], 16)
                if s.valid() and not s.routed:
                    if s.since(NSLOT + 2):
                        sp.wait_ge(d_y, 2 * GROUPS * (s.n - 1))
                    sp.dma_start(acc[:, s.par], s.tokens(h2_rows)).then_inc(ld_h2[s.par], 16)

            slots(sp, step)
            for i in range(2):
                sp.wait_ge(st_y[i], 16 * NALL // 2)

        def phase2_pe(pe):
            pe.wait_ge(d_route, ROUTE * B // 2)
            pe.wait_ge(sb_xlnT, B)
            pe.matmul(cnt_ps, ones[0:N, :], cmask[:, 0, 0], start=True, stop=True).then_inc(ps_cnt, 1)
            phase1_over(pe)
            pe.wait_ge(init_v, 4)

            def step(at):
                s = at(1)
                if s.valid():
                    pe.wait_ge(sb_T, 3 * s.n + 3)
                    pe.wait_ge(w1_hi, 2 * s.wn + 2)
                    pe.wait_ge(w1_lo, 2 * s.wn + 2)
                    for m in range(MH):
                        if m >= 3:
                            pe.wait_ge(sb_h, 2 * (MH * s.n + m - 2))
                        elif s.since(1):
                            pe.wait_ge(sb_h, 2 * (MH * (s.n - 1) + m + 4))
                        for n, (wt, w, c) in enumerate(((w1h, 0, 2), (w1h, 1, 1), (w1h, 0, 0), (w1l, 1, 1), (w1l, 0, 0))):
                            mm = pe.matmul(banks[m % 3][:, 0:s.cols], wt[:, s.wpar, w * H + m * P:w * H + (m + 1) * P],
                                           xT[:, s.par, c, 0:s.cols], start=n == 0, stop=n == 4)
                        mm.then_inc(ps_h, 1)

                def transposed():
                    s = at(2)
                    if not s.valid():
                        return
                    pe.wait_ge(d_xs, 3 * s.n + 3)
                    for c in range(3):
                        if s.since(1):
                            pe.wait_ge(sb_T, 3 * (s.n - 1) + c + 1)
                        for g in range(GROUPS):
                            mm = pe.transpose(banks[5 + c][:, g * s.rows:(g + 1) * s.rows].bitcast(F32R),
                                              xsplit[0:s.rows, g, c * P:(c + 1) * P], identr[0:s.rows, 0:s.rows])
                        mm.then_inc(ps_T, 1)

                s = at(0)
                if s.valid():
                    pe.wait_ge(d_h, MH * s.n + MH)
                    pe.wait_ge(w2_hi, 2 * s.wn + 2)
                    pe.wait_ge(w2_lo, 2 * s.wn + 2)
                    for g in range(GROUPS):
                        if g == GROUPS - 1:
                            transposed()
                        if g >= 2:
                            pe.wait_ge(d_y, 2 * GROUPS * s.n + 2 * (g - 1))
                        elif s.since(1):
                            pe.wait_ge(d_y, 2 * GROUPS * (s.n - 1) + 2 * (g + GROUPS - 1))
                        out = banks[3 + g % 2][0:s.rows]

                        def high(k):
                            return pe.matmul(out[:, 0:2 * D], hh[:, s.par, k, g * s.rows:(g + 1) * s.rows],
                                             w2s[:, s.wpar, k].rearrange("p j d -> p (j d)"),
                                             start=k == 0, stop=k == MH - 1)

                        high(0)
                        for k in range(MH):
                            pe.matmul(out[:, 0:D], hl[:, s.par, k, g * s.rows:(g + 1) * s.rows],
                                      w2s[:, s.wpar, k, 0], start=False, stop=False)
                        for k in range(1, MH):
                            mm = high(k)
                        mm.then_inc(ps_y, 1)
                else:
                    transposed()

            slots(pe, step)

        def phase2_act(act):
            zero_rows(act, range(0, NE, 2))
            phase1_over(act)

            def step(at):
                def w1_high(n):
                    s = at(2)
                    if s.valid() and s.weights():
                        if n == 0:
                            act.wait_ge(ld_w1, 16 * s.n + 16)
                            if s.since(2):
                                act.wait_ge(ps_h, MH * (s.n - 2) + MH)
                                act.wait_ge(w1_lo, 2 * (s.n - 2) + 2)
                        act.activation(w1h[:, s.par, n * H:(n + 1) * H], w1raw[:, n * H:(n + 1) * H], ACT.Copy)\
                            .then_inc(w1_hi, 1)

                def w2_high(n):
                    s = at(1)
                    if s.valid() and s.weights():
                        if n == 0:
                            act.wait_ge(ld_w2, 16 * s.n + 16)
                            if s.since(2):
                                act.wait_ge(ps_y, GROUPS * (s.n - 1))
                                act.wait_ge(w2_lo, 2 * (s.n - 2) + 2)
                        ks = slice(n * MH // 2, (n + 1) * MH // 2)
                        act.activation(w2s[:, s.par, ks, 0], w2raw[:].rearrange("p (k d) -> p k d", k=MH)[:, ks],
                                       ACT.Copy).then_inc(w2_hi, 1)

                def relu(m):
                    s = at(1)
                    if s.valid():
                        if m == 0:
                            act.wait_ge(ld_b1[s.wpar], 16 * s.whalf + 16)
                            if s.since(2):
                                act.wait_ge(ps_y, GROUPS * (s.n - 1))
                        act.wait_ge(ps_h, MH * s.n + m + 1)
                        if m >= 2:
                            act.wait_ge(d_h, MH * s.n + m - 1)
                        elif s.since(1):
                            act.wait_ge(d_h, MH * (s.n - 1) + m + 5)
                        for to in (hf[:, m % 2], hh[:, s.par, m]):
                            act.activation(to[:, 0:s.cols], banks[m % 3][:, 0:s.cols], ACT.Relu,
                                           bias=b1[:, s.wpar, m:m + 1]).then_inc(sb_h, 1)

                s = at(1)
                if s.valid() and not s.routed:
                    act.wait_ge(d_idx, 5 * s.k + 5)
                    act.activation(gate[:, s.par, 1], gate[:, s.par, 0], ACT.Exp).then_inc(a_gate, 1)
                early = not at(0).valid()
                if early:
                    for n in range(2):
                        w1_high(n)
                for m in range(MH):
                    relu(m)
                if not early:
                    for n in range(2):
                        w1_high(n)
                w2_high(0)
                w2_high(1)
                s = at(2)
                if s.valid():
                    for c in range(3):
                        act.wait_ge(ps_T, 3 * s.n + c + 1)
                        if c == 0 and s.since(2):
                            act.wait_ge(ps_h, MH * (s.n - 2) + MH)
                        act.activation(xT[:, s.par, c, 0:s.cols], banks[5 + c][:, 0:s.cols], ACT.Copy).then_inc(sb_T, 1)

            slots(act, step)

        def phase2_pool(pool):
            phase1_over(pool)

            def step(at):
                def low(s, done, high, raw, hi, lo):
                    for i in range(2):
                        pool.wait_ge(high, 2 * s.n + i + 1)
                        pool.tensor_tensor(lo[i], raw[i], hi[i].bitcast(F32), ALU.subtract).then_inc(done, 1)

                s = at(2)
                if s.valid() and s.weights():
                    if s.since(2):
                        pool.wait_ge(ps_h, MH * (s.n - 2) + MH)
                    cuts = [slice(i * H, (i + 1) * H) for i in range(2)]
                    low(s, w1_lo, w1_hi, [w1raw[:, c] for c in cuts], [w1h[:, s.par, c] for c in cuts],
                        [w1l[:, s.par, c] for c in cuts])
                s = at(1)
                if s.valid() and s.weights():
                    if s.since(2):
                        pool.wait_ge(ps_y, GROUPS * (s.n - 1))
                    cuts = [slice(i * MH // 2, (i + 1) * MH // 2) for i in range(2)]
                    raw = w2raw[:].rearrange("p (k d) -> p k d", k=MH)
                    low(s, w2_lo, w2_hi, [raw[:, c] for c in cuts], [w2s[:, s.par, c, 0] for c in cuts],
                        [w2s[:, s.par, c, 1] for c in cuts])
                s = at(0)
                if s.valid() and not s.routed:
                    if not s.since(NSLOT + 1):
                        for i in range(2):
                            pool.wait_ge(st_y[i], 16 * NSLOT // 2)
                    pool.wait_ge(d_idx, 5 * s.k + 4)
                    if s.since(NSLOT + 2):
                        pool.wait_ge(d_acc, 8 * (s.k - 2) + 8)
                    pool.sem_inc(pool_passed, 1)
                    for k in range(2):
                        for g in range(GROUPS):
                            pool.indirect_dma_start(
                                out=ye[:, s.par, k, g], out_offset=None, in_=y_rows,
                                in_offset=bass.IndirectOffsetOnAxis(ap=gidx[:, s.par, g, k:k + 1], axis=0))\
                                .then_inc(gath[s.par][k], 16)
                s = at(1)
                if s.valid() and not s.routed:
                    if not s.since(NSLOT + 1):
                        pool.wait_ge(ld_b2[s.wpar], 16 * s.whalf + 16)
                        pool.tensor_scalar(b2s[:], b2[0:SR, s.wpar], MOE_SCALE, None, ALU.mult).then_inc(p_b2, 1)
                        pool.wait_ge(p_b2, 1)
                    pool.wait_ge(ld_h2[s.par], 16 * s.khalf + 16)
                    pool.tensor_tensor(acc[:, s.par], acc[:, s.par], b2s[:].unsqueeze(1).broadcast_to([SR, GROUPS, D]),
                                       ALU.add).then_inc(p_h2, 1)

            slots(pool, step)

        def phase2_dve(dve):
            dve.tensor_copy(identr[:], ident).then_inc(init_v, 1)
            done = [0]

            def chain(ins):
                ins.then_inc(d_tab, 1)
                done[0] += 1
                dve.wait_ge(d_tab, done[0])

            slot_no = consts[0:1, C_SLOT:C_SLOT + NSLOT]
            dve.wait_ge(ps_cnt, 1)
            chain(dve.tensor_copy(cnt[:], cnt_ps))
            chain(dve.tensor_tensor(zrow[:], cnt[0:1, :], consts[0:1, C_CAP:C_CAP + NE], ALU.add))
            chain(dve.tensor_tensor(tcmp[:], cnt[:].unsqueeze(2).broadcast_to([P, NE, NTHR]),
                                    consts[:, C_THR:C_THR + NTHR].unsqueeze(1).broadcast_to([P, NE, NTHR]), ALU.is_gt))
            chain(dve.tensor_reduce(nsl[:], tcmp[:], AX, ALU.add))
            chain(dve.tensor_tensor(tcum[:], consts[0:1, C_LE:C_BIAS].rearrange("p (e f) -> p e f", e=NE),
                                    nsl[0:1].unsqueeze(1).broadcast_to([1, NE, NE]), ALU.mult))
            chain(dve.tensor_reduce(cum[:], tcum[:], AX, ALU.add))
            chain(dve.tensor_scalar(step8[:], nsl[:], -float(TS), float(CAP), ALU.mult, ALU.add))
            chain(dve.tensor_tensor(past[:], slot_no.unsqueeze(2).broadcast_to([1, NSLOT, NE]),
                                    cum[:].unsqueeze(1).broadcast_to([1, NSLOT, NE]), ALU.is_ge))
            chain(dve.tensor_tensor(tmul[:], past[:], step8[0:1].unsqueeze(1).broadcast_to([1, NSLOT, NE]), ALU.mult))
            chain(dve.tensor_reduce(tsum[:, 0], tmul[:, :, 0:NE - 1], AX, ALU.add))
            chain(dve.scalar_tensor_tensor(out=tsum[:, 1], in0=slot_no, scalar=float(TS), in1=tsum[:, 0],
                                           op0=ALU.mult, op1=ALU.add))
            chain(dve.tensor_scalar(tsum[:, 2], past[:, :, NE - 1], -1.0, 1.0, ALU.mult, ALU.add))
            chain(dve.tensor_tensor(tsum[:, 3], tsum[:, 1], tsum[:, 2], ALU.mult))
            chain(dve.tensor_reduce(tsum[:, 4], past[:, :, 0:NE - 1], AX, ALU.add))
            chain(dve.tensor_copy(table[:, 0], tsum[:, 3]))
            chain(dve.tensor_copy(table[:, 1], tsum[:, 4]))
            assert done[0] == TAB
            phase1_over(dve)

            def step(at):
                def split_h(m):
                    s = at(1)
                    if s.valid():
                        if m == 0 and s.since(2):
                            dve.wait_ge(ps_y, GROUPS * (s.n - 1))
                        dve.wait_ge(sb_h, 2 * (MH * s.n + m) + 2)
                        dve.tensor_tensor(hl[:, s.par, m, 0:s.cols], hf[:, m % 2, 0:s.cols],
                                          hh[:, s.par, m, 0:s.cols].bitcast(F32), ALU.subtract).then_inc(d_h, 1)

                def split_x():
                    s = at(2)
                    if not s.valid():
                        return
                    dve.wait_ge(ld_xr[s.par], 16 * s.half + 16)
                    if s.since(1):
                        dve.wait_ge(ps_T, 3 * (s.n - 1) + 3)
                    dve.tensor_copy(xsplit[:, :, 0:D], xr[:, s.par]).then_inc(d_xs, 1)
                    dve.wait_ge(d_xs, 3 * s.n + 1)
                    for to, of in ((slice(D, 2 * P), slice(P, D)), (slice(2 * P, 2 * D), slice(0, P))):
                        dve.tensor_tensor(xsplit[:, :, to], xr[:, s.par, :, of], xsplit[:, :, of].bitcast(F32),
                                          ALU.subtract).then_inc(d_xs, 1)

                def accumulate(k, half):
                    s = at(0)
                    if not s.valid() or s.routed:
                        return
                    if k == 0 and half == 0:
                        dve.wait_ge(d_gate, 3 * s.k + 3)
                    if half == 0:
                        dve.wait_ge(gath[s.par][k], 16 * GROUPS * (s.khalf + 1))
                    for g in range(2 * half, 2 * half + 2):
                        if k == 0:
                            dve.wait_ge(d_y, 2 * (GROUPS * s.n + g + 1))
                        else:
                            dve.wait_ge(d_acc, 8 * s.k + 2 * half + g + 1)
                        y = ysb[0:SR, s.par, g]
                        dve.scalar_tensor_tensor(out=y, in0=ye[:, s.par, k, g],
                                                 scalar=gate[:, s.par, 3 + k, g:g + 1], in1=y,
                                                 op0=ALU.mult, op1=ALU.add).then_inc(d_acc, 1)

                def result(g):
                    s = at(0)
                    if not s.valid():
                        return
                    if g == 0:
                        if s.routed:
                            dve.wait_ge(ld_b2[s.par], 16 * s.half + 16)
                        else:
                            dve.wait_ge(p_h2, s.k + 1)
                        if s.since(2):
                            dve.wait_ge(st_y[s.par], 16 * s.half)
                    dve.wait_ge(ps_y, GROUPS * s.n + g + 1)
                    high, low = banks[3 + g % 2][0:s.rows, 0:D], banks[3 + g % 2][0:s.rows, D:2 * D]
                    if s.routed:
                        y = ysb[:, s.par, g]
                        dve.tensor_tensor(y, low, b2[:, s.par], ALU.add).then_inc(d_y, 1)
                        dve.wait_ge(d_y, 2 * (GROUPS * s.n + g) + 1)
                        dve.tensor_tensor(y, high, y, ALU.add).then_inc(d_y, 1)
                    else:
                        y = ysb[0:SR, s.par, g]
                        dve.scalar_tensor_tensor(out=y, in0=low[0:SR], scalar=MOE_SCALE, in1=acc[:, s.par, g],
                                                 op0=ALU.mult, op1=ALU.add).then_inc(d_y, 1)
                        dve.wait_ge(d_y, 2 * (GROUPS * s.n + g) + 1)
                        dve.scalar_tensor_tensor(out=y, in0=high[0:SR], scalar=MOE_SCALE, in1=y,
                                                 op0=ALU.mult, op1=ALU.add).then_inc(d_y, 1)

                def rows(part):
                    s = at(2)
                    if not s.valid() or s.routed:
                        return
                    base, regions = 5 * s.k, NE - 1
                    shape = [SR, GROUPS, 2, regions]
                    if part == 0:
                        dve.wait_ge(ld_meta[s.par], 16 * s.khalf + 16)
                        dve.tensor_tensor(behind[:], mrow[:, s.par, :, 2:4].unsqueeze(3).broadcast_to(shape),
                                          consts[0:SR, C_CAP + 1:C_CAP + NE].unsqueeze(1).unsqueeze(1)
                                          .broadcast_to(shape), ALU.is_ge).then_inc(d_idx, 1)
                    elif part == 1:
                        dve.wait_ge(d_idx, base + 1)
                        dve.tensor_tensor(behind[:], behind[:],
                                          step8[0:SR, 0:regions].unsqueeze(1).unsqueeze(1).broadcast_to(shape),
                                          ALU.mult).then_inc(d_idx, 1)
                    elif part == 2:
                        dve.wait_ge(d_idx, base + 2)
                        dve.tensor_reduce(moved[:], behind[:], AX, ALU.add).then_inc(d_idx, 1)
                    elif part == 3:
                        dve.wait_ge(d_idx, base + 3)
                        dve.tensor_tensor(gidx[:, s.par], mrow[:, s.par, :, 2:4], moved[:], ALU.subtract)\
                            .then_inc(d_idx, 1)
                        dve.tensor_tensor(gate[:, s.par, 0], mrow[:, s.par, :, 1], mrow[:, s.par, :, 0],
                                          ALU.subtract).then_inc(d_idx, 1)

                def gates(part):
                    s = at(1)
                    if not s.valid() or s.routed:
                        return
                    if part == 0:
                        dve.wait_ge(a_gate, s.k + 1)
                        dve.tensor_scalar(gate[:, s.par, 2], gate[:, s.par, 1], 1.0, None, ALU.add).then_inc(d_gate, 1)
                    elif part == 1:
                        dve.wait_ge(d_gate, 3 * s.k + 1)
                        dve.reciprocal(gate[:, s.par, 3], gate[:, s.par, 2]).then_inc(d_gate, 1)
                    elif part == 2:
                        dve.wait_ge(d_gate, 3 * s.k + 2)
                        dve.tensor_tensor(gate[:, s.par, 4], gate[:, s.par, 1], gate[:, s.par, 3], ALU.mult)\
                            .then_inc(d_gate, 1)

                for m in range(MH - 1):
                    split_h(m)
                    if m < 3:
                        rows(m)
                        gates(m)
                result(0)
                split_h(MH - 1)
                split_x()
                result(1)
                accumulate(0, 0)
                result(2)
                accumulate(1, 0)
                rows(3)
                result(3)
                accumulate(0, 1)
                accumulate(1, 1)

            slots(dve, step)

        block = ctx.enter_context(nc.Block())

        def quads(eng, step):
            for q in (-1, 0, 1):
                for u in range(4):
                    if 4 * q + u >= -4:
                        step(lambda d, q=q, u=u: Image(q, u + d), u)
            with eng.Fori(2, 15) as q:
                for u in range(4):
                    step(lambda d, q=q, u=u: Image(q, u + d, 2), u)
            for q in (15, 16):
                for u in range(4):
                    step(lambda d, q=q, u=u: Image(q, u + d), u)

        NW1 = 6

        @block.sync
        def _(sp):
            sp.dma_start(we[:], a["we"]).then_inc(ld_we, 16)

            def step(at, u):
                b = at(4)
                if b.valid():
                    if b.since(2):
                        sp.wait_ge(ps_emb, b.n - 1)
                    sp.dma_start(xin[:, b.m2], a["x"][bass.ds(b.n, 1)].rearrange("o p k n -> p (o k) n"))\
                        .then_inc(ld_x[b.m2], 16)
                b = at(-2)
                if b.valid():
                    sp.wait_ge(d_ln2, LN2 * b.n + 1)
                    sp.dma_start(h2_rows[bass.ds(b.n * N, N), :], h2[:, b.m2]).then_inc(st_h2[b.m2], 16)
                    sp.wait_ge(d_ln2, LN2 * b.n + LN2)
                    sp.dma_start(xf_rows[bass.ds(b.n * N, N), :], xf[:, b.m4]).then_inc(st_xf[b.m4], 16)
                b = at(-4)
                if b.valid() and u % 2 == 0:
                    sp.wait_ge(d_route, ROUTE * b.half + ROUTE)
                    sp.dma_start(meta_rows[bass.ds(b.n * N, 2 * N), :].rearrange("(j p) c -> p j c", j=2),
                                 meta[:, b.pair]).then_inc(st_meta[b.pair], 16)

            quads(sp, step)
            phase2_sp(sp)

        @block.tensor
        def _(pe):
            def transposes(out, of, width, n):
                for t in range(n):
                    last = pe.transpose(out[0:width, t * N:(t + 1) * N], of[:, t * width:(t + 1) * width],
                                        ident[0:N, 0:N])
                return last

            pe.wait_ge(ld_we, 16)

            def step(at, u):
                def scores(r):
                    b = at(0)
                    if not b.valid():
                        return
                    if r == 0:
                        pe.wait_ge(sb_q, NG * b.n + NG)
                        pe.wait_ge(sb_k, b.n + 1)
                        if b.since(2):
                            pe.wait_ge(sb_oT, b.n - 1)
                    if b.since(1):
                        pe.wait_ge(exps, NH * (b.n - 1) + NG * (r + 1))
                    for t in range(NG):
                        mm = pe.matmul(banks[r][0:N, t * N:(t + 1) * N], kT[32 * r:32 * r + HD, b.m2, t, :],
                                       qT[32 * r:32 * r + HD, b.m2, t, :], start=True, stop=True)
                    mm.then_inc(ps_sc, 1)

                b = at(0)
                if b.valid():
                    pe.wait_ge(d_qk, QKN * b.n + QKN)
                    transposes(banks[4], qpad[:, b.m2].rearrange("p h c -> p (h c)"), P, NG).then_inc(ps_q, 1)
                    pe.wait_ge(sb_v, b.n + 1)
                    transposes(banks[5], kpad[:, b.m2].rearrange("p h c -> p (h c)"), P, NG).then_inc(ps_k, 1)
                b = at(-3)
                if b.valid():
                    pe.wait_ge(sb_xfT, b.n + 1)
                    if at(1).valid():
                        pe.wait_ge(d_ln1, LN1 * at(1).n + 1)
                    else:
                        pe.wait_ge(sb_xlnT, B)
                        pe.wait_ge(d_lg, b.n)
                    for t in range(2):
                        mm = pe.matmul(lg_ps, xfT[:, b.m2, t, :], wr[:, t, :], start=t == 0, stop=t == 1)
                    mm.then_inc(ps_lg, 1)
                b = at(-2)
                if b.valid():
                    pe.wait_ge(sb_oT, b.n + 1)
                    if b.since(1):
                        pe.wait_ge(sb_xfT, b.n)
                    for t in range(NG):
                        mm = pe.matmul(wo_ps, oT[:, b.m2, t, :], wo[:, t, :], start=t == 0, stop=t == NG - 1)
                    mm.then_inc(ps_wo, 1)
                scores(0)
                scores(1)
                b = at(1)
                if b.valid():
                    if b.fixed and b.n == 0:
                        pe.wait_ge(ld_w, 16 * NW1)
                        pe.wait_ge(init_v, 1)
                        pe.wait_ge(init_p, 7)
                    pe.wait_ge(d_ln1, LN1 * b.n + LN1)
                    if b.since(4):
                        pe.wait_ge(d_lg, b.n - 3)
                    transposes(banks[7], xln[:, b.m2], DH, 2).then_inc(ps_xlnT, 1)
                scores(2)
                scores(3)
                b = at(1)
                if b.valid():
                    pe.wait_ge(sb_xlnT, b.n + 1)
                    if b.since(1):
                        pe.wait_ge(sb_q, NG * b.n)
                    for t in range(2):
                        mm = pe.matmul(banks[4][0:N, 0:2 * D], xlnT[:, b.m2, t, :], wqkv[:, t, 0:2 * D],
                                       start=t == 0, stop=t == 1)
                    mm.then_inc(ps_qk, 1)
                    if b.since(1):
                        pe.wait_ge(sb_k, b.n)
                    for t in range(2):
                        mm = pe.matmul(v_ps, xlnT[:, b.m2, t, :], wqkv[:, t, 2 * D:3 * D],
                                       start=t == 0, stop=t == 1)
                    mm.then_inc(ps_v, 1)
                b = at(-4)
                if b.valid() and u % 2 == 0:
                    if at(-2).valid():
                        pe.wait_ge(d_ln2, LN2 * at(-2).n + 1)
                    else:
                        pe.wait_ge(sb_xfT, B)
                    pe.wait_ge(d_route, ROUTE * b.half + 10)
                    pe.matmul(pre_ps, ones[0:N, 0:N], cmask[:, b.pair].rearrange("p j e -> p (j e)"), start=True, stop=False)
                    pe.matmul(pre_ps, tri, mask[:, b.pair].rearrange("p j e -> p (j e)"), start=False, stop=True)\
                        .then_inc(ps_pre, 1)
                b = at(-2)
                if b.valid():
                    pe.wait_ge(d_ln2, LN2 * b.n + LN2)
                    if u % 2 == 0 and b.since(2):
                        pe.wait_ge(d_route, ROUTE * at(-4).half + 11)
                    transposes(banks[6], xf[:, b.m4], DH, 2).then_inc(ps_xfT, 1)
                b = at(-1)
                if b.valid():
                    pe.wait_ge(d_v, 2 * b.n + 2)
                    if at(0).valid():
                        pe.wait_ge(exps, NH * (b.n + 1) + NG)
                    else:
                        pe.wait_ge(exps, NH * b.n + NH)
                        pe.wait_ge(sb_oT, b.n)
                    for hd in range(NH):
                        r, t = hd % 4, hd // 4
                        mm = pe.matmul(banks[0][32 * r:32 * (r + 1), t * N:(t + 1) * N], vn[:, b.m2, hd, :],
                                       probs[:, b.m2, hd, :], start=True, stop=True)
                    mm.then_inc(ps_av, 1)
                b = at(2)
                if b.valid():
                    if b.since(1):
                        pe.wait_ge(sb_xlnT, b.n)
                    pe.wait_ge(ld_x[b.m2], 16 * b.half + 16)
                    for k in range(KE):
                        mm = pe.matmul(emb_ps, xin[:, b.m2, k, :], we[:, k, :], start=k == 0, stop=k == KE - 1)
                    mm.then_inc(ps_emb, 1)

            quads(pe, step)
            phase2_pe(pe)

        @block.scalar
        def _(act):
            def copy(out, ps):
                return act.activation(out, ps, ACT.Copy)

            for to, of in ((posb, a["posb"]), (consts, a["consts"]), (gains, a["gains"]), (wqkv, a["wqkv"]), (wo, a["wo"]), (wr, a["wr"])):
                act.dma_start(to[:], of).then_inc(ld_w, 16)
            act.wait_ge(init_v, 1)
            act.wait_ge(init_p, 7)

            def step(at, u):
                b = at(0)
                if b.valid():
                    act.wait_ge(ps_q, b.n + 1)
                    if b.since(2):
                        act.wait_ge(ps_sc, 4 * (b.n - 2) + 4)
                    for t in range(NG):
                        act.activation(qT[:, b.m2, t, :], banks[4][:, t * N:(t + 1) * N], ACT.Copy,
                                       scale=gain[:, t:t + 1]).then_inc(sb_q, 1)
                    act.wait_ge(ps_k, b.n + 1)
                    copy(kT[:, b.m2].rearrange("p t n -> p (t n)"), banks[5][:, 0:NG * N]).then_inc(sb_k, 1)
                def exp(r):
                    b = at(0)
                    if not b.valid():
                        return
                    act.wait_ge(d_max, 4 * b.n + r + 1)
                    if r == 0 and b.since(2):
                        act.wait_ge(ps_av, b.n - 1)
                        act.wait_ge(d_v, 2 * (b.n - 2) + 1)
                    for t in range(NG):
                        hd = 4 * t + r
                        act.activation(probs[:, b.m2, hd, :], banks[r][0:N, t * N:(t + 1) * N], ACT.Exp,
                                       bias=negmax[:, b.m2, hd:hd + 1], accum_out=rowsum[:, b.m2, hd:hd + 1])\
                            .then_inc(exps, 1)

                b = at(1)
                if b.valid():
                    act.wait_ge(ps_xlnT, b.n + 1)
                    if b.since(2):
                        act.wait_ge(ps_v, b.n - 1)
                    copy(xlnT[0:DH, b.m2].rearrange("p t n -> p (t n)"), banks[7][0:DH, 0:2 * N]).then_inc(sb_xlnT, 1)
                for r in range(4):
                    exp(r)
                b = at(1)
                if b.valid():
                    act.wait_ge(ps_v, b.n + 1)
                    if b.since(2):
                        act.wait_ge(d_v, 2 * (b.n - 2) + 2)
                    copy(vsb[:, b.m2], v_ps).then_inc(sb_v, 1)
                b = at(-2)
                if b.valid():
                    act.wait_ge(ps_xfT, b.n + 1)
                    if b.since(2):
                        act.wait_ge(ps_lg, b.n - 1)
                    copy(xfT[:, b.m2].rearrange("p t n -> p (t n)"), banks[6][0:DH, 0:2 * N]).then_inc(sb_xfT, 1)
                b = at(-1)
                if b.valid():
                    act.wait_ge(ps_av, b.n + 1)
                    if b.since(2):
                        act.wait_ge(ps_wo, b.n - 1)
                    act.activation(oT[:, b.m2].rearrange("p t n -> p (t n)"), banks[0][:, 0:NG * N], ACT.Identity,
                                   bias=consts[:, C_BIAS:C_BIAS + 1]).then_inc(sb_oT, 1)

            quads(act, step)
            phase2_act(act)

        @block.gpsimd
        def _(pool):
            pool.memset(ones[:], 1.0).then_inc(init_p, 1)
            pool.memset(qpad[:], 0.0).then_inc(init_p, 1)
            pool.memset(kpad[:], 0.0).then_inc(init_p, 1)
            pool.wait_ge(init_p, 3)
            pool.memset(xlnT[DH:DH + 1], 1.0).then_inc(init_p, 1)
            pool.wait_ge(init_p, 4)
            pool.memset(vn[:], 0.0).then_inc(init_p, 1)
            pool.wait_ge(init_p, 5)
            pool.memset(mhalf[:], -0.5).then_inc(init_p, 1)
            pool.memset(ztile[:], 0.0).then_inc(init_p, 1)
            pool.wait_ge(init_p, 7)

            def step(at, u):
                b = at(1)
                if b.valid():
                    pool.wait_ge(d_ln1, LN1 * b.n + 4)
                    if b.since(2):
                        pool.wait_ge(d_ln1, LN1 * (b.n - 2) + 5)
                    pool.tensor_tensor(rs1[:, b.m2], ve1[:, b.m2], mhalf[:, 0:1], ALU.pow).then_inc(p_rs1, 1)
                b = at(1)
                if b.valid():
                    pool.wait_ge(d_ln1, LN1 * b.n + LN1)
                    if b.since(4):
                        pool.wait_ge(d_ln2, LN2 * (b.n - 4) + 1)
                    pool.tensor_tensor(hx[:, b.m4], h[:, b.m2], xln[:, b.m2], ALU.add).then_inc(p_hx, 1)
                b = at(-2)
                if b.valid():
                    pool.wait_ge(d_ln2, LN2 * b.n + 4)
                    pool.tensor_tensor(rs2[:, b.m2], ve2[:, b.m2], mhalf[:, 0:1], ALU.pow).then_inc(p_rs2, 1)
                b = at(1)
                if b.valid():
                    pool.wait_ge(d_qk, QKN * b.n + 5)
                    pool.tensor_tensor(rsq[:, b.m2], veq[:, b.m2], mhalf[:], ALU.pow).then_inc(p_rsq, 1)
                b = at(-4)
                if b.valid():
                    pool.wait_ge(d_route, ROUTE * b.half + ROUTE)
                    pool.sem_inc(pool_passed, 1)
                    for k in range(2):
                        pool.indirect_dma_start(
                            out=xs_rows,
                            out_offset=bass.IndirectOffsetOnAxis(ap=dest[:, b.pair, b.m2, k:k + 1], axis=0),
                            in_=xf[:, b.m4], in_offset=None).then_inc(scat[b.m4], 16)

            quads(pool, step)
            phase2_pool(pool)

        @block.vector
        def _(dve):
            dve.wait_ge(ld_w, 16 * NW1)
            dve.scalar_tensor_tensor(out=gain[:], in0=gains[:, 0], scalar=HSCALE, in1=gains[:, 1],
                                     op0=ALU.mult, op1=ALU.mult).then_inc(init_v, 1)
            dve.tensor_tensor(posb[:, 0], posb[:, 0], posb[:, 1], ALU.add).then_inc(init_v, 1)
            dve.memset(cmask[:, 0, 0], 0.0).then_inc(init_v, 1)
            dve.wait_ge(init_v, 3)
            dve.wait_ge(init_p, 7)

            def step(at, u):
                def maxima(r):
                    b = at(0)
                    if not b.valid():
                        return
                    dve.wait_ge(ps_sc, 4 * b.n + r + 1)
                    if r == 0 and b.since(2):
                        dve.wait_ge(exps, NH * (b.n - 2) + NH)
                    dve.tensor_reduce(negmax[:, b.m2, r:NH:4],
                                      banks[r][0:N, 0:NG * N].rearrange("p (t n) -> p t n", t=NG),
                                      AX, ALU.max, negate=True).then_inc(d_max, 1)

                def values(part):
                    b = at(-1)
                    if not b.valid():
                        return
                    if part == 0:
                        dve.wait_ge(exps, NH * b.n + NH)
                        dve.reciprocal(rinv[:, b.m2], rowsum[:, b.m2]).then_inc(d_v, 1)
                    else:
                        dve.wait_ge(d_v, 2 * b.n + 1)
                        dve.wait_ge(sb_v, b.n + 1)
                        if b.since(2):
                            dve.wait_ge(ps_av, b.n - 1)
                        dve.tensor_tensor(vn[:, b.m2, :, 0:HD],
                                          vsb[:, b.m2].rearrange("p (h c) -> p h c", h=NH),
                                          rinv[:, b.m2].unsqueeze(2).broadcast_to([N, NH, HD]), ALU.mult)\
                            .then_inc(d_v, 1)

                def norm(b, part, src, s, mv, ve, done, base):
                    dve.wait_ge(done, base + part)
                    if part == 0:
                        dve.bn_stats(s, src).then_inc(done, 1)
                    elif part == 1:
                        dve.sem_inc(dve_passed, 1)
                        dve.bn_aggr(mv, s).then_inc(done, 1)
                    else:
                        dve.tensor_scalar(ve, mv[:, 1:2], EPS, None, ALU.add).then_inc(done, 1)

                def first_norm(part):
                    b = at(2)
                    if not b.valid():
                        return
                    if part == 0:
                        dve.wait_ge(ps_emb, b.n + 1)
                        if b.since(2):
                            dve.wait_ge(p_hx, b.n - 1)
                        dve.tensor_tensor(h[:, b.m2], emb_ps, posb[:, 0], ALU.add).then_inc(d_ln1, 1)
                    else:
                        norm(b, part - 1, h[:, b.m2], st1[:, b.m2], mv1[:, b.m2], ve1[:, b.m2], d_ln1, LN1 * b.n + 1)

                def second_norm(part):
                    b = at(-2)
                    if not b.valid():
                        return
                    if part == 0:
                        dve.wait_ge(ps_wo, b.n + 1)
                        dve.wait_ge(p_hx, b.n + 1)
                        if b.since(2):
                            dve.wait_ge(st_h2[b.m2], 16 * b.half)
                        dve.tensor_tensor(h2[:, b.m2], wo_ps, hx[:, b.m4], ALU.add).then_inc(d_ln2, 1)
                    else:
                        if part == 1 and b.since(2):
                            dve.wait_ge(p_rs2, b.n - 1)
                        norm(b, part - 1, h2[:, b.m2], st2[:, b.m2], mv2[:, b.m2], ve2[:, b.m2], d_ln2, LN2 * b.n + 1)

                def qk_norm(part):
                    b = at(1)
                    if not b.valid():
                        return
                    if part < 2:
                        dve.wait_ge(ps_qk, b.n + 1)
                        dve.bn_stats(stq[:, b.m2, part], banks[4][0:N, part * D:(part + 1) * D]).then_inc(d_qk, 1)
                    elif part == 2:
                        dve.wait_ge(d_qk, QKN * b.n + 2)
                        dve.sem_inc(dve_passed, 1)
                        for j in range(2):
                            dve.bn_aggr(mvq[:, b.m2, j], stq[:, b.m2, j]).then_inc(d_qk, 1)
                    elif part == 3:
                        dve.wait_ge(d_qk, QKN * b.n + 4)
                        if b.since(2):
                            dve.wait_ge(p_rsq, b.n - 1)
                        dve.tensor_scalar(veq[:, b.m2], mvq[:, b.m2, :, 1], EPS, None, ALU.add).then_inc(d_qk, 1)
                    else:
                        dve.wait_ge(p_rsq, b.n + 1)
                        if b.since(2):
                            dve.wait_ge(ps_k, b.n - 1)
                        for j, pad in enumerate((qpad, kpad)):
                            dve.tensor_scalar(pad[:, b.m2, :, 0:HD],
                                              banks[4][0:N, j * D:(j + 1) * D].rearrange("p (h c) -> p h c", h=NH),
                                              mvq[:, b.m2, j, 0:1], rsq[:, b.m2, j:j + 1],
                                              ALU.subtract, ALU.mult).then_inc(d_qk, 1)

                def top_two(part):
                    b = at(-3)
                    if not b.valid() or u % 2:
                        return
                    pp, base = b.pair, ROUTE * b.half
                    if part == 0:
                        dve.wait_ge(d_lg, b.n + 1)
                        dve.sem_inc(dve_passed, 1)
                        for j in range(2):
                            dve.max(top[:, pp, j], lg[:, pp, j]).then_inc(d_route, 1)
                    elif part == 1:
                        dve.wait_ge(d_route, base + 2)
                        dve.sem_inc(dve_passed, 1)
                        for j in range(2):
                            dve.max_index(topi[:, pp, j], top[:, pp, j], lg[:, pp, j]).then_inc(d_route, 1)
                        if b.since(5):
                            dve.wait_ge(st_meta[pp], 16 * b.quad)
                        dve.tensor_copy(meta[:, pp, :, 0:2], top[:, pp, :, 0:2]).then_inc(d_route, 1)
                    elif part == 2:
                        dve.wait_ge(d_route, base + 4)
                        for j in range(2):
                            dve.tensor_tensor(hot[:, pp, j],
                                              consts[0:N, C_IOTA:C_IOTA + NE].unsqueeze(1).broadcast_to([N, 2, NE]),
                                              topi[:, pp, j, 0:2].unsqueeze(2).broadcast_to([N, 2, NE]),
                                              ALU.is_equal).then_inc(d_route, 1)
                    elif part == 3:
                        dve.wait_ge(d_route, base + 7)
                        dve.tensor_tensor(mask[:, pp], hot[:, pp, :, 0], hot[:, pp, :, 1], ALU.add)\
                            .then_inc(d_route, 1)
                    elif part == 4:
                        dve.wait_ge(d_route, base + 8)
                        dve.tensor_tensor(cmask[:, pp, 1], cmask[:, pp, 0], mask[:, pp, 0], ALU.add)\
                            .then_inc(d_route, 1)
                    else:
                        dve.wait_ge(d_route, base + 9)
                        dve.tensor_tensor(cmask[:, 1 - pp, 0], cmask[:, pp, 1], mask[:, pp, 1], ALU.add)\
                            .then_inc(d_route, 1)

                def rows(part):
                    b = at(-4)
                    if not b.valid() or u % 2:
                        return
                    pp, base = b.pair, ROUTE * b.half
                    if part == 0:
                        dve.wait_ge(ps_pre, b.half + 1)
                        dve.tensor_tensor(place[:, pp], pre_ps.rearrange("p (j e) -> p j e", j=2),
                                          consts[0:N, C_CAP:C_CAP + NE].unsqueeze(1).broadcast_to([N, 2, NE]),
                                          ALU.add).then_inc(d_route, 1)
                    elif part == 1:
                        dve.wait_ge(d_route, base + 11)
                        for j in range(2):
                            dve.tensor_tensor(picked[:, pp, j], hot[:, pp, j],
                                              place[:, pp, j].unsqueeze(1).broadcast_to([N, 2, NE]), ALU.mult)\
                                .then_inc(d_route, 1)
                    elif part == 2:
                        dve.wait_ge(d_route, base + 13)
                        if b.since(4):
                            dve.wait_ge(st_meta[pp], 16 * b.quad)
                            dve.wait_ge(scat[b.m4], 32 * b.quad)
                            dve.wait_ge(scat[b.m4 + 1], 32 * b.quad)
                        dve.tensor_reduce(meta[:, pp, :, 2:4], picked[:, pp], AX, ALU.add).then_inc(d_route, 1)
                    else:
                        dve.wait_ge(d_route, base + 14)
                        dve.tensor_copy(dest[:, pp], meta[:, pp, :, 2:4]).then_inc(d_route, 1)

                values(0)
                b = at(1)
                if b.valid():
                    dve.wait_ge(p_rs1, b.n + 1)
                    if b.since(2):
                        dve.wait_ge(ps_xlnT, b.n - 1)
                    dve.tensor_scalar(xln[:, b.m2], h[:, b.m2], mv1[:, b.m2, 0:1], rs1[:, b.m2],
                                      ALU.subtract, ALU.mult).then_inc(d_ln1, 1)
                b = at(-3)
                if b.valid():
                    dve.wait_ge(ps_lg, b.n + 1)
                    dve.tensor_copy(lg[:, b.pair, b.m2], lg_ps).then_inc(d_lg, 1)
                top_two(0)
                values(1)
                top_two(1)
                second_norm(0)
                top_two(2)
                second_norm(1)
                top_two(3)
                maxima(0)
                second_norm(2)
                top_two(4)
                second_norm(3)
                top_two(5)
                maxima(1)
                b = at(-2)
                if b.valid():
                    dve.wait_ge(p_rs2, b.n + 1)
                    if b.since(4):
                        dve.wait_ge(st_xf[b.m4], 16 * b.quad)
                        dve.wait_ge(scat[b.m4], 32 * b.quad)
                        dve.wait_ge(ps_xfT, b.n - 3)
                    dve.tensor_scalar(xf[:, b.m4], h2[:, b.m2], mv2[:, b.m2, 0:1], rs2[:, b.m2],
                                      ALU.subtract, ALU.mult).then_inc(d_ln2, 1)
                maxima(2)
                maxima(3)
                rows(0)
                qk_norm(0)
                rows(1)
                qk_norm(1)
                rows(2)
                qk_norm(2)
                rows(3)
                qk_norm(3)
                qk_norm(4)
                first_norm(0)
                first_norm(1)
                first_norm(2)
                first_norm(3)

            quads(dve, step)
            phase2_dve(dve)


def kernel(**inputs):
    import numpy as np
    import concourse.bacc as bacc
    from concourse.bass_utils import run_bass_kernel_spmd

    def f(name):
        return np.asarray(inputs[name])

    x = np.pad(f("x"), ((0, 0), (0, 0), (3, 3), (3, 3))).reshape(B, 4, 11, 13, 11, 13)
    x = x.transpose(0, 1, 3, 5, 2, 4).reshape(B, 676, N)
    x = np.pad(x, ((0, 0), (0, KE * P - 676), (0, 0))).reshape(B, KE, P, N).transpose(0, 2, 1, 3)
    we = np.pad(f("L0_tok_W").T, ((0, KE * P - 676), (0, 0))).reshape(KE, P, D).transpose(1, 0, 2)

    def with_bias(weight, bias):
        t = np.zeros((DH + 1, 2, weight.shape[0]), weight.dtype)
        t[0:DH] = weight.T.reshape(2, DH, -1).transpose(1, 0, 2)
        t[DH, 1] = bias
        return t

    wqkv = np.concatenate([with_bias(f("L0_attn_Wq"), np.zeros(D, np.float32)),
                           with_bias(f("L0_attn_Wk"), f("L0_attn_bk")),
                           with_bias(f("L0_attn_Wv"), f("L0_attn_bv"))], axis=2)
    wo = np.zeros((4, 32, NG, D), np.float32)
    wo[:, 0:HD] = f("L0_attn_Wo").T.reshape(NG, 4, HD, D).transpose(1, 2, 0, 3)
    wo[0, HD, 0] = f("L0_attn_bo")
    wo = wo.reshape(P, NG, D)
    wr = f("L0_ffn_Wr").T.reshape(2, DH, NE).transpose(1, 0, 2)
    gains = np.zeros((P, 2, NG), np.float32)
    for j, name in enumerate(("L0_attn_gq", "L0_attn_gk")):
        gains.reshape(4, 32, 2, NG)[:, 0:HD, j] = f(name).reshape(NG, 4, HD).transpose(1, 2, 0)
    posb = np.stack([f("L0_tok_pos_emb"), np.broadcast_to(f("L0_tok_b"), (N, D))], axis=1)

    w1 = np.concatenate([f("L0_ffn_W1"), f("L0_ffn_sW1")[None]]).transpose(0, 2, 1)
    w1 = np.stack([w1[:, 0:P], np.concatenate([w1[:, P:D], w1[:, P:D]], axis=1)], axis=2)
    w2 = np.concatenate([f("L0_ffn_W2"), f("L0_ffn_sW2")[None]]).transpose(0, 2, 1)
    w2 = w2.reshape(NE + 1, MH, P, D).transpose(0, 2, 1, 3)
    b1 = np.concatenate([f("L0_ffn_b1"), f("L0_ffn_sb1")[None]]).reshape(NE + 1, MH, P).transpose(0, 2, 1)
    b2 = np.concatenate([f("L0_ffn_b2"), f("L0_ffn_sb2")[None]])
    b2 = np.broadcast_to(b2[:, None], (NE + 1, P, D))

    consts = np.zeros((P, C_END), np.float32)
    consts[:, C_ID:C_ID + P] = np.eye(P)
    consts[:, C_TRI:C_TRI + P] = np.triu(np.ones((P, P)), 1)
    consts[:, C_IOTA:C_IOTA + NE] = np.arange(NE)
    consts[:, C_CAP:C_CAP + NE] = np.arange(NE) * CAP
    consts[:, C_THR:C_THR + NTHR] = np.arange(NTHR) * TS
    consts[:, C_SLOT:C_SLOT + NSLOT] = np.arange(NSLOT)
    consts[:, C_LE:C_BIAS] = np.tril(np.ones((NE, NE))).reshape(-1)

    consts[HD, C_BIAS] = 1

    arrays = {"x": x, "we": we, "wqkv": wqkv, "wo": wo, "wr": wr,
              "gains": gains, "posb": posb, "w1": w1.reshape(NE + 1, P, W1C), "w2": w2.reshape(NE + 1, P, W2C),
              "b1": b1, "b2": b2, "consts": consts}
    arrays = {f"in_{k}": np.ascontiguousarray(v) for k, v in arrays.items()}

    nc = bacc.Bacc("TRN2", target_bir_lowering=False, num_devices=1)
    a = {k[3:]: nc.dram_tensor(k, v.shape, F32, kind="ExternalInput").ap() for k, v in arrays.items()}
    a["out"] = nc.dram_tensor("out", [T, D], F32, kind="ExternalOutput").ap()
    build(nc, a)
    r = run_bass_kernel_spmd(nc, [arrays], core_ids=[0])
    return np.asarray(r.results[0]["out"]).reshape(B, N, D)
```
